# Optimizing a Trainium2 kernel written in Bass

```python
import numpy as np
import jax
import jax.numpy as jnp

def _softmax(x, axis=-1):
    return jax.nn.softmax(x, axis=axis)

def _gelu(x):
    return jax.nn.gelu(x, approximate=True)

def _silu(x):
    return jax.nn.silu(x)

def _sigmoid(x):
    return jax.nn.sigmoid(x)

def _layernorm(x, axis=-1, eps=1e-05):
    m = jnp.mean(x, axis=axis, keepdims=True)
    v = jnp.var(x, axis=axis, keepdims=True)
    return (x - m) / jnp.sqrt(v + eps)

def _scatter_add(tgt, idx, src, axis=0):
    return tgt.at[idx].add(src)

def _segment_sum(src, seg, n):
    return jax.ops.segment_sum(src, seg, n)
kernel_name = 'mk_gnn_resnorm_d1_gnn_r8_b59937'

def setup_inputs(seed: int=0):
    np.random.seed(seed)
    _w = jnp.asarray

    def _rec_inputs():
        import jax
        import jax.numpy as jnp
        _gk = jax.random.key(seed)
        x = 3.989e-05 + 0.1 * jax.random.normal(jax.random.fold_in(_gk, 1), (12500, 64), jnp.float32)
        _s = jax.random.randint(jax.random.fold_in(_gk, 2), (100000,), 0, 12500, jnp.int32)
        _d = jax.random.randint(jax.random.fold_in(_gk, 3), (100000,), 0, 12500, jnp.int32)
        _loop = jnp.arange(12500, dtype=jnp.int32)
        src = jnp.concatenate([_s, _d, _loop])
        dst = jnp.concatenate([_d, _s, _loop])
        _o = jnp.argsort(dst, stable=True)
        src = src[_o]
        dst = dst[_o]
        edge_type_64 = jax.random.randint(jax.random.fold_in(_gk, 12), (212500,), 0, 64, jnp.int32)
        return (x, src, dst, edge_type_64)
    x, src, dst, edge_type_64 = _rec_inputs()

    def _L0_gnn_setup():
        import jax, jax.numpy as jnp
        import numpy as np
        N_HOPS = 2
        NEG_SLOPE = 0.2

        def _hop(emb, head, tail, rel_e, W, N):
            a_input = jnp.concatenate([emb[head], emb[tail]], axis=-1)
            e = jnp.sum(a_input @ W * rel_e, axis=-1)
            e = jax.nn.leaky_relu(e, NEG_SLOPE)
            seg_max = jax.ops.segment_max(e, head, num_segments=N)
            ex = jnp.exp(e - seg_max[head])
            denom = jax.ops.segment_sum(ex, head, num_segments=N)
            alpha = ex / denom[head]
            agg = jax.ops.segment_sum(emb[tail] * alpha[:, None], head, num_segments=N)
            return agg + emb
        key = jax.random.key(seed)
        k1, k2, k3, k4, k5 = jax.random.split(key, 5)
        N, E, D, R = (12500, 200000, 64, 64)
        edge_index = jax.random.randint(k1, (2, E), 0, N, dtype=jnp.int64)
        edge_type = jax.random.randint(k2, (E,), 0, R, dtype=jnp.int64)
        entity_emb = jax.random.normal(k3, (N, D), dtype=jnp.float32) * 0.1
        relation_emb = jax.random.normal(k4, (R, D), dtype=jnp.float32) * 0.1
        W = jax.random.normal(k5, (2 * D, D), dtype=jnp.float32) * 0.1
        return {'edge_index': edge_index, 'edge_type': edge_type, 'entity_emb': entity_emb, 'relation_emb': relation_emb, 'W': W}
    _L0_gnn_all = _L0_gnn_setup()
    _L0_gnn_in = {k: v for k, v in _L0_gnn_all.items() if k in ('relation_emb', 'W')}
    del _L0_gnn_all
    return {'x': x, 'src': src, 'dst': dst, 'edge_type_64': edge_type_64, 'L0_gnn_relation_emb': _L0_gnn_in['relation_emb'], 'L0_gnn_W': _L0_gnn_in['W']}

def reference(x, src, dst, edge_type_64, L0_gnn_relation_emb, L0_gnn_W):
    import jax
    import jax.numpy as jnp

    def _L0_gnn_ref(edge_index, edge_type, entity_emb, relation_emb, W):
        import jax, jax.numpy as jnp
        import numpy as np
        N_HOPS = 2
        NEG_SLOPE = 0.2

        def _hop(emb, head, tail, rel_e, W, N):
            a_input = jnp.concatenate([emb[head], emb[tail]], axis=-1)
            e = jnp.sum(a_input @ W * rel_e, axis=-1)
            e = jax.nn.leaky_relu(e, NEG_SLOPE)
            seg_max = jax.ops.segment_max(e, head, num_segments=N)
            ex = jnp.exp(e - seg_max[head])
            denom = jax.ops.segment_sum(ex, head, num_segments=N)
            alpha = ex / denom[head]
            agg = jax.ops.segment_sum(emb[tail] * alpha[:, None], head, num_segments=N)
            return agg + emb
        head, tail = (edge_index[0], edge_index[1])
        N = entity_emb.shape[0]
        rel_e = relation_emb[edge_type]
        res = entity_emb
        emb = entity_emb
        for _ in range(N_HOPS):
            emb = _hop(emb, head, tail, rel_e, W, N)
            norm = jnp.maximum(jnp.linalg.norm(emb, axis=-1, keepdims=True), 1e-12)
            emb = emb / norm
            res = 0.5 * res + emb
        return res
    edge_index = jnp.stack([src, dst])
    x = _layernorm(x + _L0_gnn_ref(edge_index, edge_type_64, x, L0_gnn_relation_emb, L0_gnn_W), axis=-1)
    return x

_drawn_inputs = setup_inputs


def setup_inputs(seed=0):
    import zlib

    import numpy as np

    out = dict(_drawn_inputs(seed))
    spreads = {}
    factors = {'L0_gnn_relation_emb': 4.163, 'L0_gnn_W': 4.238}
    for name, (base, spread) in spreads.items():
        noise = np.random.default_rng([zlib.crc32(name.encode()), seed]).standard_normal(out[name].shape)
        drawn = base * np.exp(spread * noise) if base else spread * noise
        out[name] = jnp.asarray(drawn.astype(out[name].dtype))
    for name, factor in factors.items():
        out[name] = (out[name] * factor).astype(out[name].dtype)
    return out
```

```python
import concourse.bass as bass
from concourse import mybir
from contextlib import ExitStack


def gnn_kernel(nc, x, src, dst, etype, rel, W, out):
    f32, i32, bf16 = mybir.dt.float32, mybir.dt.int32, mybir.dt.bfloat16
    ALU, ACT, AX = mybir.AluOpType, mybir.ActivationFunctionType, mybir.AxisListType

    L = 128
    N, D = x.shape
    E = src.shape[0]
    T = rel.shape[0]
    HOPS = 2
    NB = -(-(N + 1) // L)
    NP = NB * L
    COLS = -(-E // (L * 64)) * 64
    EP = L * COLS
    KB = COLS // L
    NL = N - (NB - 1) * L
    NEG = -1.0e30
    FAR = float(1 << 22)
    V = D + 1
    S = V + 1

    rec = nc.dram_tensor("rec_sorted", [EP + 1, 3], i32, kind="Internal").ap()
    x_head = nc.dram_tensor("head_rows", [EP, T], f32, kind="Internal").ap()
    tq = nc.dram_tensor("tail_rows", [NP, D + T], f32, kind="Internal").ap()
    pt = nc.dram_tensor("p_rows", [NP, T], f32, kind="Internal").ap()
    states = nc.dram_tensor("edge_states", [EP, S], f32, kind="Internal").ap()

    ctx = ExitStack()
    with ctx:
        def sem(name):
            return ctx.enter_context(nc.semaphore(name))

        def sb(scope, name, shape, dt=f32):
            return scope.enter_context(nc.sbuf_tensor(name, shape, dt))

        def pb(scope, name, shape, dt=f32):
            return scope.enter_context(nc.psum_tensor(name, shape, dt))

        def reached(step, k):
            return not isinstance(step, int) or step >= k

        class Chain:

            def __init__(self, eng, s, start=0):
                self.eng, self.sem, self.n, self.base = eng, s, start, 0

            def __call__(self, ins):
                ins.then_inc(self.sem, 1)
                self.n += 1
                self.eng.wait_ge(self.sem, self.base + self.n)

        def rounds(eng, chain, n, links, body):
            body(0)
            before = chain.n
            with eng.Fori(1, n) as i:
                chain.base = (i - 1) * links
                body(i)
                assert chain.n == before + links, chain.n - before
            chain.n, chain.base = before + (n - 1) * links, 0

        ident = sb(ctx, "ident", [L, L])
        identb = sb(ctx, "identb", [L, L], bf16)
        iotab = sb(ctx, "iotab", [L, L], bf16)
        iotaf = sb(ctx, "iotaf", [L, T])
        trif = sb(ctx, "trif", [L, L])
        trib = sb(ctx, "trib", [L, L], bf16)
        onesf = sb(ctx, "onesf", [L, L])
        pbase = sb(ctx, "pbase", [L, 1])
        base = sb(ctx, "base", [L, NB])
        cnt = sb(ctx, "cnt", [L, NB])
        startix = sb(ctx, "startix", [L, NB], i32)
        endix = sb(ctx, "endix", [L, NB], i32)
        has = sb(ctx, "has", [L, NB])
        emb = sb(ctx, "emb", [L, NB, D])
        wqp = sb(ctx, "wqp", [D, 2 * T])

        dve_links, act_links, pe_links, pool_links = (sem(n) for n in ("dve_links", "act_links", "pe_links", "pool_links"))
        turns = sem("pool_turns")
        chain_at = {"dve": 0, "act": 0, "pool": 0}

        early = ExitStack()
        recc = sb(early, "recc", [L, COLS, 3], i32)
        hl = sb(early, "hl", [L, COLS], bf16)
        hb = sb(early, "hb", [L, COLS], bf16)
        with ExitStack() as s1:
            raw = sb(s1, "raw", [L, 3, KB, L], i32)
            rawf = sb(s1, "rawf", [L, 3, KB, L])
            hint = sb(s1, "hint", [L, 2, COLS], i32)
            cols = sb(s1, "cols", [L, 3, COLS])
            w1 = sb(s1, "w1", [D, 3, D])
            wT = sb(s1, "wT", [D, 3, D])
            before = sb(s1, "before", [1, 3], i32)
            psA = [pb(s1, f"psA{k}", [L, 4 * L]) for k in range(4)]
            psw = pb(s1, "psw", [D, 4 * L])
            pads, loads, const, rawf_ok, tr_ok, ev_ok, cols_ok = (sem(n) for n in (
                "pads", "loads", "const", "rawf_ok", "tr_ok", "ev_ok", "cols_ok"))
            NT = 3 * KB
            GT = -(-NT // 4)
            full = (KB - 1) * L * L
            rows, rest = divmod(E - full, L)
            block = s1.enter_context(nc.Block())

            @block.sync
            def _(sp):
                sp.wait_ge(pads, 5)
                n = 0
                for k, a in enumerate((dst, etype, src)):
                    sp.dma_start(raw[:, k, 0:KB - 1, :], a[0:full].rearrange("(k c e) -> c k e", c=L, e=L)).then_inc(loads, 16)
                    sp.dma_start(raw[0:rows, k, KB - 1, :], a[full:full + rows * L].rearrange("(c e) -> c e", e=L)).then_inc(loads, 16)
                    n += 2
                    if rest:
                        sp.dma_start(raw[rows:rows + 1, k, KB - 1, 0:rest], a[E - rest:E].rearrange("(c e) -> c e", c=1)).then_inc(loads, 16)
                        n += 1
                sp.dma_start(emb[:, 0:NB - 1, :], x[0:(NB - 1) * L, :].rearrange("(b p) d -> p b d", p=L)).then_inc(loads, 16)
                sp.dma_start(emb[0:NL, NB - 1, :], x[(NB - 1) * L:N, :]).then_inc(loads, 16)
                sp.dma_start(w1[:, 0, :], W[D:2 * D, :]).then_inc(loads, 16)
                sp.dma_start(w1[:, 1, :], W[0:D, :]).then_inc(loads, 16)
                sp.dma_start(w1[0:T, 2, :], rel).then_inc(loads, 16)
                sp.dma_start(rec[0:1, :], before[:, :]).then_inc(loads, 16)
                n += 6
                sp.wait_ge(loads, 16 * n)

            n_loads = 16 * (3 * (3 if rest else 2) + 6)

            @block.gpsimd
            def _(gp):
                nc.gpsimd.memset(raw[:, 0:2, KB - 1, :], 0).then_inc(pads, 1)
                nc.gpsimd.memset(raw[:, 2, KB - 1, :], N).then_inc(pads, 1)
                nc.gpsimd.memset(emb[:, NB - 1, :], 0.0).then_inc(pads, 1)
                nc.gpsimd.memset(before[:, :], -1).then_inc(pads, 1)
                nc.gpsimd.memset(onesf[:, :], 1.0).then_inc(pads, 1)
                gp.wait_ge(pads, 5)
                nc.gpsimd.affine_select(out=ident[:, :], in_=onesf[:, :], pattern=[[-1, L]], compare_op=ALU.is_equal,
                                        fill=0.0, base=0, channel_multiplier=1).then_inc(const, 1)
                nc.gpsimd.affine_select(out=trif[:, :], in_=onesf[:, :], pattern=[[1, L]], compare_op=ALU.is_gt,
                                        fill=0.0, base=0, channel_multiplier=-1).then_inc(const, 1)
                nc.gpsimd.iota(iotab[:, :], pattern=[[1, L]], base=0, channel_multiplier=0,
                               allow_small_or_imprecise_dtypes=True).then_inc(const, 1)
                nc.gpsimd.iota(iotaf[:, :], pattern=[[1, T]], base=0, channel_multiplier=0,
                               allow_small_or_imprecise_dtypes=True).then_inc(const, 1)
                nc.gpsimd.iota(pbase[:, :], pattern=[[0, 1]], base=0, channel_multiplier=COLS,
                               allow_small_or_imprecise_dtypes=True).then_inc(const, 1)

            @block.tensor
            def _(pe):
                pe.wait_ge(const, 5)
                pe.wait_ge(rawf_ok, 1)
                for g in range(GT):
                    if g >= 4:
                        pe.wait_ge(ev_ok, g - 3)
                    for t in range(4 * g, min(4 * g + 4, NT)):
                        last = nc.tensor.transpose(psA[g % 4][:, (t % 4) * L:(t % 4 + 1) * L],
                                                   rawf[:, t // KB, t % KB, :], ident[:, :])
                    last.then_inc(tr_ok, 1)
                for k in range(3):
                    last = nc.tensor.transpose(psw[:, k * D:(k + 1) * D], w1[:, k, :], ident[0:D, 0:D])
                last.then_inc(tr_ok, 1)
                pe.wait_ge(ev_ok, GT + 1)
                nc.tensor.matmul(psw[:, 0:T], wT[:, 0, :], wT[:, 2, :], start=True, stop=True)
                nc.tensor.matmul(psw[:, T:2 * T], wT[:, 1, :], wT[:, 2, :], start=True, stop=True).then_inc(tr_ok, 1)

            @block.scalar
            def _(act):
                flat = cols[:, :, :].rearrange("p k c -> p (k c)")
                for g in range(GT):
                    act.wait_ge(tr_ok, g + 1)
                    w = min(4 * L, NT * L - 4 * L * g)
                    nc.scalar.copy(flat[:, 4 * L * g:4 * L * g + w], psA[g % 4][:, 0:w]).then_inc(ev_ok, 1)
                act.wait_ge(tr_ok, GT + 1)
                nc.scalar.copy(wT[:, :, :].rearrange("p k c -> p (k c)"), psw[:, 0:3 * D]).then_inc(ev_ok, 1)
                act.wait_ge(tr_ok, GT + 2)
                nc.scalar.copy(wqp[:, :], psw[:, 0:2 * T]).then_inc(cols_ok, 1)

            @block.vector
            def _(dve):
                link = Chain(dve, dve_links)
                dve.wait_ge(const, 5)
                nc.vector.tensor_copy(identb[:, :], ident[:, :])
                nc.vector.tensor_copy(trib[:, :], trif[:, :])
                dve.wait_ge(loads, n_loads)
                nc.vector.tensor_copy(rawf[:, :, :, :], raw[:, :, :, :]).then_inc(rawf_ok, 1)
                dve.wait_ge(ev_ok, GT)
                link(nc.vector.tensor_copy(recc[:, :, :], cols[:, :, :].rearrange("p k c -> p c k")))
                link(nc.vector.tensor_scalar(hint[:, 0, :], recc[:, :, 2], L - 1, None, ALU.bitwise_and))
                link(nc.vector.tensor_scalar(hint[:, 1, :], recc[:, :, 2], L.bit_length() - 1, None, ALU.logical_shift_right))
                nc.vector.tensor_copy(hl[:, :], hint[:, 0, :])
                nc.vector.tensor_copy(hb[:, :], hint[:, 1, :])
                dve.wait_ge(cols_ok, 1)
                chain_at["dve"] = link.n

        Q4 = COLS // 4
        HR = Q4 // 8
        ohl = sb(early, "ohl", [L, 4, 4, L], bf16)
        ohb = sb(early, "ohb", [L, 4, 4, NB], bf16)
        ring_r = sb(early, "ring_r", [L, 4, 4, NB])

        def one_hots(q, r):
            nc.vector.tensor_tensor(ohl[:, r, :, :], iotab[:, :].unsqueeze(1).to_broadcast([L, 4, L]),
                                    hl[:, bass.ds(4 * q, 4)].unsqueeze(2).to_broadcast([L, 4, L]), ALU.is_equal)
            return nc.vector.tensor_tensor(ohb[:, r, :, :], iotab[:, 0:NB].unsqueeze(1).to_broadcast([L, 4, NB]),
                                           hb[:, bass.ds(4 * q, 4)].unsqueeze(2).to_broadcast([L, 4, NB]), ALU.is_equal)

        x_zero = sem("x_zero")
        zeros = sb(early, "zeros", [L, 32 * T])
        ZR = COLS // 32
        with ExitStack() as s2:
            psc = pb(s2, "psc", [L, NB])
            psb = pb(s2, "psb", [L, 2, NB])
            tot = sb(s2, "tot", [L, NB])
            tot1 = sb(s2, "tot1", [L, NB + 1])
            tmp2 = sb(s2, "tmp2", [L, NB])
            z_ok, oh_ok, h_used, h_all, cnt_ok, pre_ok = (sem(n) for n in ("z_ok", "oh_ok", "h_used", "h_all", "cnt_ok", "pre_ok"))
            block = s2.enter_context(nc.Block())
            xz = x_head.rearrange("(p j) t -> p (j t)", p=L)

            @block.sync
            def _(sp):
                sp.wait_ge(z_ok, 1)
                with sp.Fori(0, ZR) as i:
                    sp.dma_start(xz[:, bass.ds(i * 32 * T, 32 * T)], zeros[:, :]).then_inc(x_zero, 16)

            @block.vector
            def _(dve):
                link = Chain(dve, dve_links, chain_at["dve"])
                nc.vector.memset(zeros[:, :], 0.0).then_inc(z_ok, 1)

                def body(i):
                    for u in range(8):
                        q = 8 * i + u
                        if reached(q, 4):
                            dve.wait_ge(h_used, q - 3)
                        one_hots(q, u % 4).then_inc(oh_ok, 1)
                rounds(dve, link, HR, 0, body)
                dve.wait_ge(h_all, 1)
                link(nc.vector.tensor_copy(cnt[:, :], psc[:, :]))
                nc.vector.tensor_copy(tmp2[:, :], cnt[:, :]).then_inc(cnt_ok, 1)
                dve.wait_ge(pre_ok, 1)
                link(nc.vector.memset(tot1[:, 0:1], 1.0))
                link(nc.vector.tensor_copy(tot[:, :], psb[:, 1, :]))
                link(nc.vector.tensor_tensor_scan(tot1[:, 1:NB + 1], onesf[:, 0:NB], tot[:, :], tot1[:, 0:1], ALU.mult, ALU.add))
                link(nc.vector.tensor_tensor(base[:, :], psb[:, 0, :], tot1[:, 0:NB], ALU.add))
                link(nc.vector.tensor_scalar(has[:, :], cnt[:, :], 1.0, None, ALU.min))
                link(nc.vector.tensor_scalar(tmp2[:, :], has[:, :], -FAR, FAR - 1.0, ALU.mult, ALU.add))
                link(nc.vector.tensor_tensor(tmp2[:, :], tmp2[:, :], base[:, :], ALU.add))
                link(nc.vector.tensor_copy(startix[:, :], tmp2[:, :]))
                link(nc.vector.tensor_tensor(tmp2[:, :], base[:, :], cnt[:, :], ALU.add))
                link(nc.vector.tensor_scalar(tmp2[:, :], tmp2[:, :], -2.0, 0.0, ALU.add, ALU.max))
                link(nc.vector.tensor_copy(endix[:, :], tmp2[:, :]))
                link(nc.vector.tensor_copy(ring_r[:, 3, 3, :], base[:, :]))
                chain_at["dve"] = link.n

            @block.tensor
            def _(pe):
                def body(i):
                    for u in range(8):
                        q = 8 * i + u
                        pe.wait_ge(oh_ok, q + 1)
                        for c in range(4):
                            last = nc.tensor.matmul(psc[:, :], ohl[:, u % 4, c, :], ohb[:, u % 4, c, :],
                                                    start=isinstance(i, int) and i == 0 and u == 0 and c == 0,
                                                    stop=isinstance(i, int) and i == HR - 1 and u == 7 and c == 3)
                        last.then_inc(h_used, 1)
                body(0)
                with pe.Fori(1, HR - 1) as i:
                    body(i)
                body(HR - 1)
                pe.wait_ge(h_used, Q4)
                nc.tensor.nop().then_inc(h_all, 1)
                pe.wait_ge(cnt_ok, 1)
                nc.tensor.matmul(psb[:, 0, :], trif[:, :], cnt[:, :], start=True, stop=True)
                nc.tensor.matmul(psb[:, 1, :], onesf[:, :], cnt[:, :], start=True, stop=True).then_inc(pre_ok, 1)

        with ExitStack() as s3:
            oTb = sb(s3, "oTb", [L, 4, 4, L], bf16)
            oTc = sb(s3, "oTc", [NB, 4, 4, L], bf16)
            oTf = sb(s3, "oTf", [L, 4, 4, L])
            prior = sb(s3, "prior", [L, 2, 4, L], bf16)
            masked = sb(s3, "masked", [L, 4, NB])
            rank = sb(s3, "rank", [L, 4])
            rankix = sb(s3, "rankix", [L, 2, 16], i32)
            recst = sb(s3, "recst", [L, 2, 16, 3], i32)
            psT = [pb(s3, f"psT{k}", [L, 2, 4, L], bf16) for k in range(2)]
            psS = [pb(s3, f"psS{k}", [L, 4, L]) for k in range(2)]
            psG = [pb(s3, f"psG{k}", [L, 4, L]) for k in range(2)]
            psH = [pb(s3, f"psH{k}", [L, 4, L]) for k in range(2)]
            oh2, t_ok, h_ok, same_ok, g_ok, oT_ok, r_ok, s_ok, m_ok, grp_ok = (sem(n) for n in (
                "oh2", "t_ok", "h_ok", "same_ok", "g_ok", "oT_ok", "r_ok", "s_ok", "m_ok", "grp_ok"))
            scat = [sem(f"scat{k}") for k in range(2)]
            RR = Q4 // 8
            block = s3.enter_context(nc.Block())

            @block.vector
            def _(dve):
                link = Chain(dve, dve_links, chain_at["dve"])

                def counts(q, u):
                    dve.wait_ge(h_ok, q + 1)
                    if reached(q, 1):
                        dve.wait_ge(r_ok, q)
                    nc.vector.tensor_tensor(ring_r[:, u % 4, :, :], psH[u % 2][:, :, 0:NB],
                                            ring_r[:, (u - 1) % 4, 3:4, :].to_broadcast([L, 4, NB]), ALU.add).then_inc(r_ok, 1)

                def priors(q, u):
                    dve.wait_ge(same_ok, q + 1)
                    nc.vector.scalar_tensor_tensor(prior[:, u % 2, :, :], psS[u % 2][:, :, :], 2.0,
                                                   trib[:, :].unsqueeze(1).to_broadcast([L, 4, L]),
                                                   ALU.is_equal, ALU.mult).then_inc(s_ok, 1)

                def ranks(q, u, rounds_done):
                    par, k = (u // 4) % 2, u % 4
                    if k == 0:
                        if reached(q, 8):
                            dve.wait_ge(scat[par], rounds_done)
                        nc.vector.tensor_copy(recst[:, par, :, :].rearrange("p c k -> p (c k)"),
                                              recc[:, bass.ds(4 * q, 16), :].rearrange("p c k -> p (c k)"))
                    dve.wait_ge(g_ok, q + 1)
                    link(nc.vector.tensor_tensor(masked[:, :, :], psG[u % 2][:, :, 0:NB], ohb[:, u % 4, :, :], ALU.mult))
                    m_ok_ins = nc.vector.tensor_reduce(rank[:, :], masked[:, :, :], AX.X, ALU.add)
                    m_ok_ins.then_inc(m_ok, 1)
                    dve.wait_ge(m_ok, q + 1)
                    last = nc.vector.tensor_copy(rankix[:, par, 4 * k:4 * k + 4], rank[:, :])
                    if k == 3:
                        last.then_inc(grp_ok, 1)

                def body(i):
                    for u in range(8):
                        q = 8 * i + u
                        one_hots(q, u % 4).then_inc(oh2, 1)
                        if reached(q, 1):
                            counts(q - 1, u - 1)
                        if reached(q, 2):
                            priors(q - 2, u - 2)
                        if reached(q, 3):
                            ranks(q - 3, u - 3, 256 * i)

                rounds(dve, link, RR, 8, body)
                counts(Q4 - 1, 7)
                priors(Q4 - 2, 6)
                ranks(Q4 - 3, 5, None)
                priors(Q4 - 1, 7)
                ranks(Q4 - 2, 6, None)
                ranks(Q4 - 1, 7, None)
                chain_at["dve"] = link.n

            @block.tensor
            def _(pe):
                def flip(q, u):
                    pe.wait_ge(oh2, q + 1)
                    for c in range(4):
                        nc.tensor.transpose(psT[u % 2][:, 0, c, :], ohl[:, u % 4, c, :], identb[:, :])
                        last = nc.tensor.transpose(psT[u % 2][0:NB, 1, c, :], ohb[:, u % 4, c, :], identb[:, :])
                    last.then_inc(t_ok, 1)

                def hist(q, u):
                    if reached(q, 2):
                        pe.wait_ge(r_ok, q - 1)
                    for c in range(4):
                        for b in range(c + 1):
                            last = nc.tensor.matmul(psH[u % 2][:, c, 0:NB], ohl[:, u % 4, b, :], ohb[:, u % 4, b, :],
                                                    start=b == 0, stop=b == c)
                    last.then_inc(h_ok, 1)

                def same(q, u):
                    pe.wait_ge(oT_ok, q + 1)
                    for c in range(4):
                        nc.tensor.matmul(psS[u % 2][:, c, :], oTb[:, u % 4, c, :], oTb[:, u % 4, c, :], start=True, stop=False)
                        last = nc.tensor.matmul(psS[u % 2][:, c, :], oTc[:, u % 4, c, :], oTc[:, u % 4, c, :], start=False, stop=True)
                    last.then_inc(same_ok, 1)

                def candidates(q, u):
                    pe.wait_ge(s_ok, q + 1)
                    pe.wait_ge(r_ok, q + 1)
                    if reached(q, 2):
                        pe.wait_ge(m_ok, q - 1)
                    for c in range(4):
                        r = ring_r[:, u % 4, c - 1, :] if c else ring_r[:, (u - 1) % 4, 3, :]
                        nc.tensor.matmul(psG[u % 2][:, c, 0:NB], oTf[:, u % 4, c, :], r, start=True, stop=False)
                        last = nc.tensor.matmul(psG[u % 2][:, c, 0:NB], prior[:, u % 2, c, :], ohb[:, u % 4, c, :], start=False, stop=True)
                    last.then_inc(g_ok, 1)

                def body(i):
                    for u in range(8):
                        q = 8 * i + u
                        flip(q, u)
                        hist(q, u)
                        if reached(q, 1):
                            same(q - 1, u - 1)
                        if reached(q, 2):
                            candidates(q - 2, u - 2)
                body(0)
                with pe.Fori(1, RR) as i:
                    body(i)
                same(Q4 - 1, 7)
                candidates(Q4 - 2, 6)
                candidates(Q4 - 1, 7)

            @block.scalar
            def _(act):
                def body(i):
                    for u in range(8):
                        q = 8 * i + u
                        act.wait_ge(t_ok, q + 1)
                        if reached(q, 4):
                            act.wait_ge(g_ok, q - 3)
                        nc.scalar.copy(oTb[:, u % 4, :, :], psT[u % 2][:, 0, :, :])
                        nc.scalar.copy(oTc[:, u % 4, :, :], psT[u % 2][0:NB, 1, :, :])
                        nc.scalar.copy(oTf[:, u % 4, :, :], psT[u % 2][:, 0, :, :]).then_inc(oT_ok, 1)
                body(0)
                with act.Fori(1, RR) as i:
                    body(i)

            @block.gpsimd
            def _(gp):
                with gp.Fori(0, RR) as i:
                    for g in range(2):
                        gp.wait_ge(grp_ok, 2 * i + g + 1)
                        gp.sem_inc(turns, 1)
                        for c in range(16):
                            nc.gpsimd.indirect_dma_start(
                                rec, bass.IndirectOffsetOnAxis(ap=rankix[:, g, c:c + 1], axis=0),
                                recst[:, g, c, :], None, bounds_check=EP, oob_is_err=False).then_inc(scat[g], 16)
                for g in range(2):
                    gp.wait_ge(scat[g], 256 * RR)
        early.close()

        late = ExitStack()
        tails = sb(late, "tails", [L, COLS], i32)
        types = sb(late, "types", [L, COLS])
        keep = sb(late, "keep", [L, COLS])
        neg = sb(late, "neg", [L, COLS])
        fixix = sb(late, "fixix", [L, 1], i32)
        hfirst = sb(late, "hfirst", [L, 1], i32)
        cutT = sb(late, "cutT", [S, L])
        res = sb(late, "res", [L, NB, D])
        with ExitStack() as s4:
            recs = sb(s4, "recs", [L, COLS + 1, 3], i32)
            jota = sb(s4, "jota", [L, COLS])
            m1 = sb(s4, "m1", [L, 4])
            cut = sb(s4, "cut", [L, S])
            psx = pb(s4, "psx", [L, L])
            rl, jo, cut_ok, cutT_ok = (sem(n) for n in ("rl", "jo", "cut_ok", "cutT_ok"))
            block = s4.enter_context(nc.Block())

            @block.sync
            def _(sp):
                sp.dma_start(recs[:, 0:COLS, :], rec[0:EP, :].rearrange("(p j) k -> p j k", p=L)).then_inc(rl, 16)
                sp.dma_start(recs[:, COLS, :], rec[1:EP + 1, :].rearrange("(p j) k -> p j k", p=L)[:, COLS - 1, :]).then_inc(rl, 16)
                sp.wait_ge(rl, 32)
                sp.wait_ge(x_zero, 16 * ZR)

            @block.gpsimd
            def _(gp):
                nc.gpsimd.iota(jota[:, :], pattern=[[1, COLS]], base=0, channel_multiplier=0,
                               allow_small_or_imprecise_dtypes=True).then_inc(jo, 1)

            @block.vector
            def _(dve):
                link = Chain(dve, dve_links, chain_at["dve"])
                dve.wait_ge(rl, 32)
                nc.vector.tensor_copy(tails[:, :], recs[:, 1:COLS + 1, 0])
                nc.vector.tensor_copy(types[:, :], recs[:, 1:COLS + 1, 1])
                nc.vector.tensor_copy(hfirst[:, :], recs[:, 1, 2:3])
                link(nc.vector.tensor_tensor(keep[:, :], recs[:, 1:COLS + 1, 2], recs[:, 0:COLS, 2], ALU.is_equal))
                link(nc.vector.tensor_scalar(neg[:, :], keep[:, :], -NEG, NEG, ALU.mult, ALU.add))
                dve.wait_ge(jo, 1)
                link(nc.vector.scalar_tensor_tensor(jota[:, :], keep[:, :], float(COLS), jota[:, :], ALU.mult, ALU.add))
                link(nc.vector.tensor_reduce(m1[:, 0:1], jota[:, 1:COLS], AX.X, ALU.min))
                link(nc.vector.tensor_scalar(m1[:, 1:2], m1[:, 0:1], float(COLS), -1.0, ALU.min, ALU.add))
                link(nc.vector.tensor_tensor(m1[:, 2:3], m1[:, 1:2], pbase[:, :], ALU.add))
                link(nc.vector.tensor_copy(fixix[:, :], m1[:, 2:3]))
                link(nc.vector.tensor_reduce(m1[:, 3:4], neg[:, :], AX.X, ALU.min))
                link(nc.vector.tensor_copy(cut[:, :], m1[:, 3:4].to_broadcast([L, S])))
                nc.vector.memset(res[:, :, :], 0.0).then_inc(cut_ok, 1)
                dve.wait_ge(cutT_ok, 1)
                link(nc.vector.tensor_copy(cutT[:, :], psx[0:S, :]))
                link(nc.vector.tensor_copy(res[:, :, :], emb[:, :, :]))
                chain_at["dve"] = link.n

            @block.tensor
            def _(pe):
                pe.wait_ge(cut_ok, 1)
                nc.tensor.transpose(psx[0:S, :], cut[:, :], ident[:, :]).then_inc(cutT_ok, 1)

        J = 16
        B = COLS // J
        BR = B // 4
        tqw, node_T, node_e, node_m, node_q = (sem(n) for n in ("tqw", "node_T", "node_e", "node_m", "node_q"))
        psc_sem, pcar = sem("p_scattered"), sem("p_carried")
        ix_ok, pin_ok, a_ok, ae_ok, gfree, st_ok, or_ok, m_set, z_set = (sem(n) for n in (
            "ix_ok", "pin_ok", "a_ok", "ae_ok", "gfree", "st_ok", "or_ok", "m_set", "z_set"))
        gath = [sem(f"gath{k}") for k in range(4)]
        xl = [sem(f"xl{k}") for k in range(2)]
        so = [sem(f"so{k}") for k in range(2)]
        tl_ok, tlT_ok, aw2_ok, ex2_ok, cv_ok, cvT_ok, fx, d_ok, e2_ok, fix_ok, rows_ok, sq_ok, sr_ok, out_ok, y_ok = (sem(n) for n in (
            "tl_ok", "tlT_ok", "aw2_ok", "ex2_ok", "cv_ok", "cvT_ok", "fx", "d_ok", "e2_ok", "fix_ok", "rows_ok", "sq_ok", "sr_ok", "out_ok", "y_ok"))
        tail_state = sb(late, "tail_state", [L, S])
        pcarry = sb(late, "pcarry", [L, T])
        NG = 7
        NS = NB // NG
        for hop in range(HOPS):
            with ExitStack() as s5:
                eT = sb(s5, f"eT{hop}", [D, 2, NG, L])
                qs = sb(s5, f"qs{hop}", [L, NB, T])
                ps = sb(s5, f"ps{hop}", [L, NB, T])
                psE = [pb(s5, f"psE{hop}{k}", [L, 8, L]) for k in range(2)]
                psQ = [pb(s5, f"psQ{hop}{k}", [L, 8, 2 * T]) for k in range(2)]
                block = s5.enter_context(nc.Block())

                @block.tensor
                def _(pe):
                    def project(g):
                        pe.wait_ge(node_e, hop * NS + g + 1)
                        if g >= 2:
                            pe.wait_ge(node_q, hop * NS + g - 1)
                        for k in range(NG):
                            last = nc.tensor.matmul(psQ[g % 2][:, k, :], eT[:, g % 2, k, :], wqp[:, :], start=True, stop=True)
                        last.then_inc(node_m, 1)
                    for g in range(NS):
                        if g >= 2:
                            pe.wait_ge(node_e, hop * NS + g - 1)
                        for k in range(NG):
                            last = nc.tensor.transpose(psE[g % 2][0:D, k, :], emb[:, g * NG + k, :], ident[:, :])
                        last.then_inc(node_T, 1)
                        if g:
                            project(g - 1)
                    project(NS - 1)

                @block.scalar
                def _(act):
                    for g in range(NS):
                        act.wait_ge(node_T, hop * NS + g + 1)
                        if g >= 2:
                            act.wait_ge(node_m, hop * NS + g - 1)
                        nc.scalar.copy(eT[:, g % 2, :, :], psE[g % 2][0:D, 0:NG, :]).then_inc(node_e, 1)

                @block.vector
                def _(dve):
                    for g in range(NS):
                        dve.wait_ge(node_m, hop * NS + g + 1)
                        nc.vector.tensor_copy(ps[:, g * NG:(g + 1) * NG, :], psQ[g % 2][:, 0:NG, T:2 * T])
                        nc.vector.tensor_copy(qs[:, g * NG:(g + 1) * NG, :], psQ[g % 2][:, 0:NG, 0:T]).then_inc(node_q, 1)

                @block.sync
                def _(sp):
                    sp.dma_start(tq[:, 0:D].rearrange("(b p) d -> p b d", p=L), emb[:, :, :]).then_inc(tqw, 16)
                    sp.wait_ge(node_q, NS * (hop + 1))
                    sp.dma_start(pt.rearrange("(b p) d -> p b d", p=L), ps[:, :, :]).then_inc(tqw, 16)
                    sp.dma_start(tq[:, D:D + T].rearrange("(b p) d -> p b d", p=L), qs[:, :, :]).then_inc(tqw, 16)
                    sp.wait_ge(tqw, 48 * (hop + 1))

                @block.gpsimd
                def _(gp):
                    for b in range(NB):
                        if b % NG == 0:
                            gp.wait_ge(node_q, hop * NS + b // NG + 1)
                        nc.gpsimd.indirect_dma_start(
                            x_head, bass.IndirectOffsetOnAxis(ap=startix[:, b:b + 1], axis=0), ps[:, b, :], None,
                            bounds_check=EP - 1, oob_is_err=False).then_inc(psc_sem, 16)
                    gp.wait_ge(tqw, 48 * (hop + 1))
                    nc.gpsimd.indirect_dma_start(
                        pcarry[:, :], None, pt, bass.IndirectOffsetOnAxis(ap=hfirst[:, 0:1], axis=0),
                        bounds_check=NP - 1, oob_is_err=False).then_inc(pcar, 16)
                    gp.wait_ge(pcar, 16 * (hop + 1))
                    gp.wait_ge(psc_sem, 16 * NB * (hop + 1))

            with ExitStack() as s6:
                ix = sb(s6, f"ix{hop}", [L, 4, J], i32)
                G = sb(s6, f"G{hop}", [L, 4, J, D + T])
                Xb = sb(s6, f"Xb{hop}", [L, 2, J, T])
                Pin = sb(s6, f"Pin{hop}", [L, 2, T, J + 1])
                KE = sb(s6, f"KE{hop}", [L, 2, T, J + 1])
                Pex = sb(s6, f"Pex{hop}", [L, 2, T, J + 1])
                U = sb(s6, f"U{hop}", [L, J, T])
                OHt = sb(s6, f"OHt{hop}", [L, J, T])
                er = sb(s6, f"er{hop}", [L, J])
                el = sb(s6, f"el{hop}", [L, J])
                Mx = sb(s6, f"Mx{hop}", [L, 4, J + 1])
                dd = sb(s6, f"dd{hop}", [L, J])
                aw = sb(s6, f"aw{hop}", [L, 2, 2, J])
                ew = sb(s6, f"ew{hop}", [L, 2, 2, J])
                WR = sb(s6, f"WR{hop}", [L, V, J + 1])
                AE = sb(s6, f"AE{hop}", [L, 2, V, J + 1])
                ST = sb(s6, f"ST{hop}", [L, 2, V, J + 1])
                OR = sb(s6, f"OR{hop}", [L, 2, J, S])
                block = s6.enter_context(nc.Block())
                hb0 = hop * B
                hr0 = hop * BR
                xv = x_head.rearrange("(p j) t -> p j t", p=L)
                sv = states.rearrange("(p j) t -> p j t", p=L)

                @block.sync
                def _(sp):
                    def load(b, u, i):
                        if reached(b, 2):
                            sp.wait_ge(pin_ok, hb0 + b - 1)
                        sp.dma_start(Xb[:, u % 2, :, :], xv[:, bass.ds(b * J, J), :]).then_inc(xl[u % 2], 16)

                    def store(b, u, i):
                        sp.wait_ge(or_ok, hb0 + b + 1)
                        sp.dma_start(sv[:, bass.ds(b * J, J), :], OR[:, u % 2, :, :]).then_inc(so[u % 2], 16)
                    load(0, 0, 0)

                    def body(i, last=False):
                        for u in range(4):
                            b = 4 * i + u
                            if not (last and u == 3):
                                load(b + 1, u + 1, i)
                            if reached(b, 2):
                                store(b - 2, u - 2, i)
                    body(0)
                    with sp.Fori(1, BR - 1) as i:
                        body(i)
                    body(BR - 1, True)
                    store(B - 2, 2, 0)
                    store(B - 1, 3, 0)
                    for k in range(2):
                        sp.wait_ge(so[k], 16 * (B // 2) * (hop + 1))

                @block.gpsimd
                def _(gp):
                    def body(i):
                        for u in range(4):
                            b = 4 * i + u
                            if reached(b, 4):
                                gp.wait_ge(gfree, hb0 + b - 3)
                                gp.sem_inc(turns, 1)
                            gp.wait_ge(ix_ok, hb0 + b + 1)
                            gp.sem_inc(turns, 1)
                            for j in range(J):
                                nc.gpsimd.indirect_dma_start(
                                    G[:, u, j, :], None, tq, bass.IndirectOffsetOnAxis(ap=ix[:, u, j:j + 1], axis=0),
                                    bounds_check=NP - 1, oob_is_err=False).then_inc(gath[u], 16)
                    body(0)
                    with gp.Fori(1, BR) as i:
                        body(i)

                @block.scalar
                def _(act):
                    def pin(b, u, i):
                        act.wait_ge(xl[u % 2], 16 * (hr0 * 2 + 2 * i + u // 2 + 1))
                        nc.scalar.copy(Pin[:, u % 2, :, 1:J + 1], Xb[:, u % 2, :, :].rearrange("p j t -> p t j"))
                        nc.scalar.copy(KE[:, u % 2, :, 1:J + 1],
                                       keep[:, bass.ds(b * J, J)].unsqueeze(1).to_broadcast([L, T, J])).then_inc(pin_ok, 1)

                    def weigh(b, u):
                        act.wait_ge(a_ok, hb0 + b + 1)
                        nc.scalar.activation(ew[:, u % 2, :, :], aw[:, u % 2, :, :], ACT.Exp).then_inc(m_set, 1)
                        act.wait_ge(m_set, hb0 + b + 1)
                        nc.scalar.copy(AE[:, u % 2, :, 1:J + 1],
                                       ew[:, u % 2, 0:1, :].to_broadcast([L, V, J])).then_inc(ae_ok, 1)

                    def pack(b, u, i):
                        act.wait_ge(st_ok, hb0 + b + 1)
                        if reached(b, 2):
                            act.wait_ge(so[u % 2], 16 * (hr0 * 2 + 2 * i + u // 2))
                        nc.scalar.copy(OR[:, u % 2, :, 0:V], ST[:, u % 2, :, 1:J + 1].rearrange("p f j -> p j f"))
                        nc.scalar.copy(OR[:, u % 2, :, V], Mx[:, u % 4, 1:J + 1]).then_inc(or_ok, 1)

                    def body(i):
                        for u in range(4):
                            b = 4 * i + u
                            pin(b, u, i)
                            if reached(b, 1):
                                weigh(b - 1, u - 1)
                            if reached(b, 2):
                                pack(b - 2, u - 2, i)
                    act.wait_ge(z_set, hop + 1)
                    body(0)
                    with act.Fori(1, BR) as i:
                        body(i)
                    weigh(B - 1, 3)
                    pack(B - 2, 2, BR - 1)
                    pack(B - 1, 3, BR - 1)

                @block.vector
                def _(dve):
                    link = Chain(dve, dve_links, chain_at["dve"])

                    def stage_ix(b, u):
                        nc.vector.tensor_copy(ix[:, u % 4, :], tails[:, bass.ds(b * J, J)]).then_inc(ix_ok, 1)

                    def logits(b, u, i):
                        p, pp = u % 2, (u - 1) % 2
                        dve.wait_ge(pin_ok, hb0 + b + 1)
                        link(nc.vector.tensor_copy(Pin[:, p, :, 0:1],
                                                   Pex[:, pp, :, J:J + 1] if reached(b, 1) else pcarry[:, :].unsqueeze(2)))
                        flat = lambda a: a[:, p, :, :].rearrange("p t j -> p (t j)")
                        nc.vector.tensor_tensor_scan(flat(Pex), flat(KE), flat(Pin), 0.0, ALU.mult, ALU.add)
                        link(nc.vector.tensor_tensor(OHt[:, :, :], iotaf[:, :].unsqueeze(1).to_broadcast([L, J, T]),
                                                     types[:, bass.ds(b * J, J)].unsqueeze(2).to_broadcast([L, J, T]), ALU.is_equal))
                        dve.wait_ge(gath[u], 16 * J * (hr0 + i + 1))
                        link(nc.vector.tensor_tensor(U[:, :, :], Pex[:, p, :, 1:J + 1].rearrange("p t j -> p j t"),
                                                     G[:, u, :, D:D + T], ALU.add))
                        link(nc.vector.tensor_tensor(U[:, :, :], U[:, :, :], OHt[:, :, :], ALU.mult))
                        link(nc.vector.tensor_reduce(er[:, :], U[:, :, :], AX.X, ALU.add))
                        link(nc.vector.scalar_tensor_tensor(el[:, :], er[:, :], 0.2, er[:, :], ALU.mult, ALU.max))
                        link(nc.vector.tensor_copy(Mx[:, u, 0:1], Mx[:, (u - 1) % 4, J:J + 1]))
                        link(nc.vector.tensor_tensor_scan(Mx[:, u, 1:J + 1], neg[:, bass.ds(b * J, J)], el[:, :],
                                                          Mx[:, u, 0:1], ALU.add, ALU.max))
                        link(nc.vector.tensor_tensor(dd[:, :], Mx[:, u, 0:J], neg[:, bass.ds(b * J, J)], ALU.add))
                        nc.vector.tensor_tensor(aw[:, p, 0, :], dd[:, :], Mx[:, u, 1:J + 1], ALU.subtract)
                        nc.vector.tensor_tensor(aw[:, p, 1, :], el[:, :], Mx[:, u, 1:J + 1], ALU.subtract).then_inc(a_ok, 1)

                    def sums(b, u):
                        p, pp = u % 2, (u - 1) % 2
                        dve.wait_ge(ae_ok, hb0 + b + 1)
                        nc.vector.tensor_tensor(WR[:, 0:D, 1:J + 1], G[:, u % 4, :, 0:D].rearrange("p j f -> p f j"),
                                                ew[:, p, 1:2, :].to_broadcast([L, D, J]), ALU.mult).then_inc(gfree, 1)
                        nc.vector.tensor_copy(WR[:, D, 1:J + 1], ew[:, p, 1, :])
                        link(nc.vector.tensor_copy(WR[:, :, 0:1], ST[:, pp, :, J:J + 1]))
                        dve.wait_ge(gfree, hb0 + b + 1)
                        flat = lambda a: a[:, p, :, :].rearrange("p t j -> p (t j)")
                        nc.vector.tensor_tensor_scan(flat(ST), flat(AE), WR[:, :, :].rearrange("p t j -> p (t j)"),
                                                     0.0, ALU.mult, ALU.add).then_inc(st_ok, 1)
                        dve.wait_ge(st_ok, hb0 + b + 1)

                    def body(i, last=False):
                        for u in range(4):
                            b = 4 * i + u
                            if not (last and u >= 2):
                                stage_ix(b + 2, u + 2)
                            logits(b, u, i)
                            if reached(b, 1):
                                sums(b - 1, u - 1)

                    nc.vector.memset(Mx[:, 3, :], NEG)
                    nc.vector.memset(ST[:, 1, :, :], 0.0)
                    for k in range(2):
                        nc.vector.memset(KE[:, k, :, 0:1], 0.0)
                        link(nc.vector.memset(AE[:, k, :, 0:1], 0.0))
                    nc.vector.memset(dd[:, 0:1], 0.0).then_inc(z_set, 1)
                    stage_ix(0, 0)
                    stage_ix(1, 1)
                    body(0)
                    before = link.n
                    LINKS = 4 * 10
                    with dve.Fori(1, BR - 1) as i:
                        link.base = (i - 1) * LINKS
                        body(i)
                        assert link.n == before + LINKS, link.n - before
                    link.n, link.base = before + (BR - 2) * LINKS, 0
                    body(BR - 1, True)
                    sums(B - 1, 3)
                    nc.vector.tensor_copy(tail_state[:, 0:V], ST[:, 1, :, J])
                    nc.vector.tensor_copy(tail_state[:, V:S], Mx[:, 3, J:J + 1])
                    link(nc.vector.memset(dd[:, 0:1], 0.0))
                    chain_at["dve"] = link.n

            with ExitStack() as s7:
                mbc = sb(s7, f"mbc{hop}", [L, S])
                tT = sb(s7, f"tT{hop}", [S, L])
                mT = sb(s7, f"mT{hop}", [S, L])
                MC = sb(s7, f"MC{hop}", [S, L + 1])
                CV = sb(s7, f"CV{hop}", [S, L + 1])
                aw2 = sb(s7, f"aw2{hop}", [S, 2, L])
                ew2 = sb(s7, f"ew2{hop}", [S, 2, L])
                carr = sb(s7, f"carr{hop}", [L, S])
                mcar = sb(s7, f"mcar{hop}", [L, 1])
                fr = sb(s7, f"fr{hop}", [L, S])
                mm = sb(s7, f"mm{hop}", [L, 3])
                me = sb(s7, f"me{hop}", [L, 2])
                R = sb(s7, f"R{hop}", [L, NB, S])
                tmp = sb(s7, f"tmp{hop}", [L, NB, D])
                st = sb(s7, f"st{hop}", [L, 4, NB])
                psm = pb(s7, f"psm{hop}", [L, 4, L])
                block = s7.enter_context(nc.Block())

                @block.tensor
                def _(pe):
                    pe.wait_ge(tl_ok, hop + 1)
                    nc.tensor.transpose(psm[0:S, 0, :], tail_state[:, :], ident[:, :])
                    nc.tensor.transpose(psm[0:S, 1, :], mbc[:, :], ident[:, :]).then_inc(tlT_ok, 1)
                    pe.wait_ge(cv_ok, hop + 1)
                    nc.tensor.transpose(psm[:, 2, 0:S], CV[:, 0:L], ident[0:S, 0:S])
                    nc.tensor.transpose(psm[:, 3, 0:S], MC[:, 0:L], ident[0:S, 0:S]).then_inc(cvT_ok, 1)

                @block.scalar
                def _(act):
                    act.wait_ge(aw2_ok, hop + 1)
                    nc.scalar.activation(ew2[:, :, :], aw2[:, :, :], ACT.Exp).then_inc(ex2_ok, 1)
                    act.wait_ge(d_ok, hop + 1)
                    nc.scalar.activation(me[:, :], mm[:, 1:3], ACT.Exp).then_inc(e2_ok, 1)
                    act.wait_ge(sq_ok, hop + 1)
                    nc.scalar.activation(st[:, 2, :], st[:, 1, :], ACT.Sqrt).then_inc(sr_ok, 1)
                    if hop == HOPS - 1:
                        act.wait_ge(sq_ok, hop + 2)
                        nc.scalar.activation(st[:, 2, :], st[:, 1, :], ACT.Sqrt).then_inc(sr_ok, 1)

                @block.gpsimd
                def _(gp):
                    nc.gpsimd.indirect_dma_start(
                        fr[:, :], None, states, bass.IndirectOffsetOnAxis(ap=fixix[:, 0:1], axis=0),
                        bounds_check=EP - 1, oob_is_err=False).then_inc(fx, 16)
                    gp.wait_ge(fix_ok, hop + 1)
                    nc.gpsimd.indirect_dma_start(
                        states, bass.IndirectOffsetOnAxis(ap=fixix[:, 0:1], axis=0), fr[:, :], None,
                        bounds_check=EP - 1, oob_is_err=False).then_inc(fx, 16)
                    gp.wait_ge(fx, 32 * (hop + 1))
                    for b in range(NB):
                        nc.gpsimd.indirect_dma_start(
                            R[:, b, :], None, states, bass.IndirectOffsetOnAxis(ap=endix[:, b:b + 1], axis=0),
                            bounds_check=EP - 1, oob_is_err=False).then_inc(rows_ok, 16)

                @block.vector
                def _(dve):
                    link = Chain(dve, dve_links, chain_at["dve"])
                    nc.vector.tensor_copy(mbc[:, :], tail_state[:, V:S].to_broadcast([L, S])).then_inc(tl_ok, 1)
                    dve.wait_ge(tlT_ok, hop + 1)
                    nc.vector.tensor_copy(tT[:, :], psm[0:S, 0, :])
                    nc.vector.tensor_copy(mT[:, :], psm[0:S, 1, :])
                    nc.vector.memset(CV[:, 0:1], 0.0)
                    link(nc.vector.memset(MC[:, 0:1], NEG))
                    link(nc.vector.tensor_tensor_scan(MC[:, 1:L + 1], cutT[:, :], mT[:, :], MC[:, 0:1], ALU.add, ALU.max))
                    link(nc.vector.tensor_tensor(aw2[:, 0, :], MC[:, 0:L], cutT[:, :], ALU.add))
                    link(nc.vector.tensor_tensor(aw2[:, 0, :], aw2[:, 0, :], MC[:, 1:L + 1], ALU.subtract))
                    nc.vector.tensor_tensor(aw2[:, 1, :], mT[:, :], MC[:, 1:L + 1], ALU.subtract).then_inc(aw2_ok, 1)
                    dve.wait_ge(ex2_ok, hop + 1)
                    link(nc.vector.tensor_tensor(tT[:, :], tT[:, :], ew2[:, 1, :], ALU.mult))
                    nc.vector.tensor_tensor_scan(CV[:, 1:L + 1], ew2[:, 0, :], tT[:, :], CV[:, 0:1], ALU.mult, ALU.add).then_inc(cv_ok, 1)
                    dve.wait_ge(cvT_ok, hop + 1)
                    nc.vector.tensor_copy(carr[:, :], psm[:, 2, 0:S])
                    link(nc.vector.tensor_tensor(mcar[:, :], psm[:, 3, 0:1], neg[:, 0:1], ALU.add))
                    dve.wait_ge(fx, 32 * hop + 16)
                    link(nc.vector.tensor_tensor(mm[:, 0:1], fr[:, V:S], mcar[:, :], ALU.max))
                    nc.vector.tensor_tensor(mm[:, 1:2], fr[:, V:S], mm[:, 0:1], ALU.subtract)
                    nc.vector.tensor_tensor(mm[:, 2:3], mcar[:, :], mm[:, 0:1], ALU.subtract).then_inc(d_ok, 1)
                    dve.wait_ge(e2_ok, hop + 1)
                    link(nc.vector.tensor_scalar(carr[:, 0:V], carr[:, 0:V], me[:, 1:2], None, ALU.mult))
                    link(nc.vector.scalar_tensor_tensor(fr[:, 0:V], fr[:, 0:V], me[:, 0:1], carr[:, 0:V], ALU.mult, ALU.add))
                    nc.vector.tensor_copy(fr[:, V:S], mm[:, 0:1]).then_inc(fix_ok, 1)
                    dve.wait_ge(rows_ok, 16 * NB * (hop + 1))
                    link(nc.vector.reciprocal(st[:, 0, :], R[:, :, D]))
                    link(nc.vector.tensor_tensor(st[:, 0, :], st[:, 0, :], has[:, :], ALU.mult))
                    link(nc.vector.tensor_tensor(tmp[:, :, :], R[:, :, 0:D], st[:, 0, :].unsqueeze(2).to_broadcast([L, NB, D]), ALU.mult))
                    link(nc.vector.tensor_tensor(emb[:, :, :], emb[:, :, :], tmp[:, :, :], ALU.add))

                    def square_sum(a):
                        link(nc.vector.tensor_tensor(tmp[:, :, :], a[:, :, :], a[:, :, :], ALU.mult))
                        link(nc.vector.tensor_reduce(st[:, 3, :], tmp[:, :, :], AX.X, ALU.add))
                    square_sum(emb)
                    nc.vector.tensor_scalar(st[:, 1, :], st[:, 3, :], 1e-24, None, ALU.max).then_inc(sq_ok, 1)
                    dve.wait_ge(sr_ok, hop + 1)
                    link(nc.vector.reciprocal(st[:, 0, :], st[:, 2, :]))
                    link(nc.vector.tensor_tensor(emb[:, :, :], emb[:, :, :], st[:, 0, :].unsqueeze(2).to_broadcast([L, NB, D]), ALU.mult))
                    link(nc.vector.scalar_tensor_tensor(res[:, :, :].rearrange("p b d -> p (b d)"), res[:, :, :].rearrange("p b d -> p (b d)"), 0.5,
                                                        emb[:, :, :].rearrange("p b d -> p (b d)"), ALU.mult, ALU.add))
                    if hop == HOPS - 1:
                        dve.wait_ge(y_ok, 32)
                        xr = R[:, :, :].rearrange("p b s -> p (b s)")[:, 0:NB * D].rearrange("p (b d) -> p b d", d=D)
                        link(nc.vector.tensor_tensor(res[:, :, :], res[:, :, :], xr, ALU.add))
                        link(nc.vector.tensor_reduce(st[:, 0, :], res[:, :, :], AX.X, ALU.add))
                        link(nc.vector.tensor_scalar(st[:, 0, :], st[:, 0, :], 1.0 / D, None, ALU.mult))
                        link(nc.vector.tensor_tensor(res[:, :, :], res[:, :, :], st[:, 0, :].unsqueeze(2).to_broadcast([L, NB, D]), ALU.subtract))
                        square_sum(res)
                        nc.vector.tensor_scalar(st[:, 1, :], st[:, 3, :], 1.0 / D, 1e-5, ALU.mult, ALU.add).then_inc(sq_ok, 1)
                        dve.wait_ge(sr_ok, hop + 2)
                        link(nc.vector.reciprocal(st[:, 0, :], st[:, 2, :]))
                        nc.vector.tensor_tensor(res[:, :, :], res[:, :, :], st[:, 0, :].unsqueeze(2).to_broadcast([L, NB, D]), ALU.mult).then_inc(out_ok, 1)
                    chain_at["dve"] = link.n

                if hop == HOPS - 1:
                    @block.sync
                    def _(sp):
                        sp.wait_ge(sr_ok, HOPS)
                        xr = R[:, :, :].rearrange("p b s -> p (b s)")[:, 0:NB * D].rearrange("p (b d) -> p b d", d=D)
                        sp.dma_start(xr[:, 0:NB - 1, :], x[0:(NB - 1) * L, :].rearrange("(b p) d -> p b d", p=L)).then_inc(y_ok, 16)
                        sp.dma_start(xr[0:NL, NB - 1, :], x[(NB - 1) * L:N, :]).then_inc(y_ok, 16)
                        sp.wait_ge(out_ok, 1)
                        sp.dma_start(out[0:(NB - 1) * L, :].rearrange("(b p) d -> p b d", p=L), res[:, 0:NB - 1, :]).then_inc(y_ok, 16)
                        sp.dma_start(out[(NB - 1) * L:N, :], res[0:NL, NB - 1, :]).then_inc(y_ok, 16)
                        sp.wait_ge(y_ok, 64)
        late.close()


_INS = ["x", "src", "dst", "edge_type_64", "L0_gnn_relation_emb", "L0_gnn_W"]


def kernel(**inputs):
    import numpy as _np
    import concourse.bacc as _bacc
    from concourse import mybir as _mybir
    from concourse.bass_utils import run_bass_kernel_spmd as _run

    nc = _bacc.Bacc("TRN2", target_bir_lowering=False, num_devices=1)
    arrays, args = {}, []
    for name in _INS:
        a = _np.ascontiguousarray(inputs[name])
        arrays[f"in_{name}_dram"] = a
        args.append(nc.dram_tensor(f"in_{name}_dram", a.shape, _mybir.dt.from_np(a.dtype), kind="ExternalInput").ap())
    shape = inputs["x"].shape
    out = nc.dram_tensor("out_dram", shape, _mybir.dt.float32, kind="ExternalOutput").ap()
    gnn_kernel(nc, *args, out)
    r = _run(nc, [arrays], core_ids=[0])
    return r.results[0]["out_dram"]
```

```python
import concourse.bass as bass
from concourse import mybir
from contextlib import ExitStack


def gnn_kernel(nc, x, src, dst, etype, rel, W, out):
    f32, i32, bf16 = mybir.dt.float32, mybir.dt.int32, mybir.dt.bfloat16
    ALU, ACT, AX = mybir.AluOpType, mybir.ActivationFunctionType, mybir.AxisListType

    L = 128
    N, D = x.shape
    E = src.shape[0]
    T = rel.shape[0]
    HOPS = 2
    NB = -(-(N + 1) // L)
    NP = NB * L
    COLS = -(-E // (L * 64)) * 64
    EP = L * COLS
    KB = COLS // L
    NL = N - (NB - 1) * L
    NEG = -1.0e30
    FAR = float(1 << 22)
    V = D + 1
    S = V + 1

    rec = nc.dram_tensor("rec_sorted", [EP + 1, 3], i32, kind="Internal").ap()
    x_head = nc.dram_tensor("head_rows", [EP, T], f32, kind="Internal").ap()
    tq = nc.dram_tensor("tail_rows", [NP, D + T], f32, kind="Internal").ap()
    pt = nc.dram_tensor("p_rows", [NP, T], f32, kind="Internal").ap()
    states = nc.dram_tensor("edge_states", [EP, S], f32, kind="Internal").ap()

    ctx = ExitStack()
    with ctx:
        def sem(name):
            return ctx.enter_context(nc.semaphore(name))

        def sb(scope, name, shape, dt=f32):
            return scope.enter_context(nc.sbuf_tensor(name, shape, dt))

        def pb(scope, name, shape, dt=f32):
            return scope.enter_context(nc.psum_tensor(name, shape, dt))

        def reached(step, k):
            return not isinstance(step, int) or step >= k

        class Chain:

            def __init__(self, eng, s, start=0):
                self.eng, self.sem, self.n, self.base = eng, s, start, 0

            def __call__(self, ins):
                ins.then_inc(self.sem, 1)
                self.n += 1
                self.eng.wait_ge(self.sem, self.base + self.n)

        def rounds(eng, chain, n, links, body):
            body(0)
            before = chain.n
            with eng.Fori(1, n) as i:
                chain.base = (i - 1) * links
                body(i)
                assert chain.n == before + links, chain.n - before
            chain.n, chain.base = before + (n - 1) * links, 0

        ident = sb(ctx, "ident", [L, L])
        identb = sb(ctx, "identb", [L, L], bf16)
        iotab = sb(ctx, "iotab", [L, L], bf16)
        iotaf = sb(ctx, "iotaf", [L, T])
        trif = sb(ctx, "trif", [L, L])
        trib = sb(ctx, "trib", [L, L], bf16)
        onesf = sb(ctx, "onesf", [L, L])
        pbase = sb(ctx, "pbase", [L, 1])
        base = sb(ctx, "base", [L, NB])
        cnt = sb(ctx, "cnt", [L, NB])
        startix = sb(ctx, "startix", [L, NB], i32)
        endix = sb(ctx, "endix", [L, NB], i32)
        has = sb(ctx, "has", [L, NB])
        emb = sb(ctx, "emb", [L, NB, D])
        wqp = sb(ctx, "wqp", [D, 2 * T])
        psc_sem, pcar, hf_ok, six_ok = sem("p_scattered"), sem("p_carried"), sem("hf_ok"), sem("six_ok")
        pcarry = sb(ctx, "pcarry", [L, T])
        tail_state = sb(ctx, "tail_state", [L, S])
        tmp3 = sb(ctx, "tmp3", [L, NB])
        tails = sb(ctx, "tails", [L, COLS], i32)
        types = sb(ctx, "types", [L, COLS])
        keep = sb(ctx, "keep", [L, COLS])
        neg = sb(ctx, "neg", [L, COLS])
        fixix = sb(ctx, "fixix", [L, 1], i32)
        hfirst = sb(ctx, "hfirst", [L, 1], i32)
        cutT = sb(ctx, "cutT", [S, L])
        res = sb(ctx, "res", [L, NB, D])

        dve_links, act_links, pe_links, pool_links = (sem(n) for n in ("dve_links", "act_links", "pe_links", "pool_links"))
        turns, pe_turns = sem("pool_turns"), sem("pe_turns")
        chain_at = {"dve": 0, "act": 0, "pool": 0}

        tables = ExitStack()
        ps = sb(tables, "ps0", [L, NB, T])
        early = ExitStack()
        recc = sb(early, "recc", [L, COLS, 3], i32)
        hl = sb(early, "hl", [L, COLS], bf16)
        hb = sb(early, "hb", [L, COLS], bf16)
        Q4 = COLS // 4
        HR = Q4 // 8
        ohl = sb(early, "ohl", [L, 4, 4, L], bf16)
        ohb = sb(early, "ohb", [L, 4, 4, NB], bf16)
        ring_r = sb(early, "ring_r", [L, 4, 4, NB])
        zeros = sb(early, "zeros", [L, 32 * T])
        x_zero = sem("x_zero")
        tqw, node_T, node_e, node_m, node_q = (sem(n) for n in ("tqw", "node_T", "node_e", "node_m", "node_q"))
        ZR = COLS // 32
        LP = E // COLS
        LW = LP - LP % 16
        REST = E - LP * COLS
        with ExitStack() as s1:
            raw = sb(s1, "raw", [L, 3, COLS], i32)
            hint = sb(s1, "hint", [L, 2, COLS], i32)
            w1 = sb(s1, "w1", [D, 3, D])
            wT = sb(s1, "wT", [D, 3, D])
            before = sb(s1, "before", [1, 3], i32)
            iota2 = sb(s1, "iota2", [L, L, 2], bf16)
            pairl = sb(s1, "pairl", [L, 4, 2, L, 2], bf16)
            pairb = sb(s1, "pairb", [L, 4, 2, NB, 2], bf16)
            tot = sb(s1, "tot", [L, NB])
            tot1 = sb(s1, "tot1", [L, NB + 1])
            tmp2 = sb(s1, "tmp2", [L, NB])
            stage = sb(s1, "stage", [L, 2, D])
            eT = sb(s1, "eT", [D, 2, L])
            qs = res
            psw = pb(s1, "psw", [D, 4 * L])
            psc = pb(s1, "psc", [L, 4 * L])
            psb = pb(s1, "psb", [L, 4, L])
            psE = pb(s1, "psE", [D, 4, L])
            psQ = pb(s1, "psQ", [L, 4, 2 * T])
            pads, hloads, loads, const, tr_ok, ev_ok, wqp_ok, stg_ok = (sem(n) for n in (
                "pads", "hloads", "loads", "const", "tr_ok", "ev_ok", "wqp_ok", "stg_ok"))
            z_ok, oh_ok, h_used, cnt_ok, pre_ok, recc_ok = (sem(n) for n in ("z_ok", "oh_ok", "h_used", "cnt_ok", "pre_ok", "recc_ok"))
            NPARTS = 2 + (REST > 0)
            n_loads = 6 + 2 * NPARTS
            block = s1.enter_context(nc.Block())
            xz = x_head.rearrange("(p j) t -> p (j t)", p=L)

            @block.sync
            def _(sp):
                def edges(k, a, s):
                    sp.dma_start(raw[0:LW, k, :], a[0:LW * COLS].rearrange("(p j) -> p j", j=COLS)).then_inc(s, 16)
                    sp.dma_start(raw[LW:LP, k, :], a[LW * COLS:LP * COLS].rearrange("(p j) -> p j", j=COLS)).then_inc(s, 16)
                    if REST:
                        sp.dma_start(raw[LP:LP + 1, k, 0:REST], a[LP * COLS:E].rearrange("(p j) -> p j", p=1)).then_inc(s, 16)
                sp.wait_ge(pads, 5)
                edges(2, src, hloads)
                sp.dma_start(w1[:, 0, :], W[D:2 * D, :]).then_inc(loads, 16)
                sp.dma_start(w1[:, 1, :], W[0:D, :]).then_inc(loads, 16)
                sp.dma_start(w1[0:T, 2, :], rel).then_inc(loads, 16)
                sp.dma_start(emb[:, 0:NB - 1, :], x[0:(NB - 1) * L, :].rearrange("(b p) d -> p b d", p=L)).then_inc(loads, 16)
                sp.dma_start(emb[0:NL, NB - 1, :], x[(NB - 1) * L:N, :]).then_inc(loads, 16)
                edges(0, dst, loads)
                edges(1, etype, loads)
                sp.dma_start(rec[0:1, :], before[:, :]).then_inc(loads, 16)
                sp.wait_ge(z_ok, 1)
                with sp.Fori(0, ZR) as i:
                    sp.dma_start(xz[:, bass.ds(i * 32 * T, 32 * T)], zeros[:, :]).then_inc(x_zero, 16)
                sp.wait_ge(loads, 16 * n_loads)
                sp.dma_start(tq[:, 0:D].rearrange("(b p) d -> p b d", p=L), emb[:, :, :]).then_inc(tqw, 16)
                sp.wait_ge(node_q, NB // 2)
                sp.dma_start(pt.rearrange("(b p) d -> p b d", p=L), ps[:, :, :]).then_inc(tqw, 16)
                sp.dma_start(tq[:, D:D + T].rearrange("(b p) d -> p b d", p=L), qs[:, :, :]).then_inc(tqw, 16)
                sp.wait_ge(tqw, 48)

            @block.gpsimd
            def _(gp):
                nc.gpsimd.memset(emb[:, NB - 1, :], 0.0).then_inc(pads, 1)
                nc.gpsimd.memset(before[:, :], -1).then_inc(pads, 1)
                nc.gpsimd.iota(iota2[:, :, :], pattern=[[1, L], [0, 2]], base=0, channel_multiplier=0,
                               allow_small_or_imprecise_dtypes=True).then_inc(const, 1)
                nc.gpsimd.memset(onesf[:, :], 1.0).then_inc(pads, 1)
                gp.wait_ge(pads, 5)
                nc.gpsimd.affine_select(out=ident[:, :], in_=onesf[:, :], pattern=[[-1, L]], compare_op=ALU.is_equal,
                                        fill=0.0, base=0, channel_multiplier=1).then_inc(const, 1)
                nc.gpsimd.affine_select(out=trif[:, :], in_=onesf[:, :], pattern=[[1, L]], compare_op=ALU.is_gt,
                                        fill=0.0, base=0, channel_multiplier=-1).then_inc(const, 1)
                nc.gpsimd.iota(iotab[:, :], pattern=[[1, L]], base=0, channel_multiplier=0,
                               allow_small_or_imprecise_dtypes=True).then_inc(const, 1)
                nc.gpsimd.iota(iotaf[:, :], pattern=[[1, T]], base=0, channel_multiplier=0,
                               allow_small_or_imprecise_dtypes=True).then_inc(const, 1)
                nc.gpsimd.iota(pbase[:, :], pattern=[[0, 1]], base=0, channel_multiplier=COLS,
                               allow_small_or_imprecise_dtypes=True).then_inc(const, 1)
                gp.wait_ge(hloads, 16 * NPARTS)
                gp.wait_ge(loads, 16 * n_loads)
                for k in range(3):
                    nc.gpsimd.tensor_copy(recc[:, :, k], raw[:, k, :]).then_inc(recc_ok, 1)

            @block.tensor
            def _(pe):
                pe.wait_ge(const, 6)
                pe.wait_ge(loads, 16 * n_loads)
                for k in range(3):
                    last = nc.tensor.transpose(psw[:, k * D:(k + 1) * D], w1[:, k, :], ident[0:D, 0:D])
                last.then_inc(tr_ok, 1)
                pe.wait_ge(ev_ok, 1)
                nc.tensor.matmul(psw[:, 0:T], wT[:, 0, :], wT[:, 2, :], start=True, stop=True)
                nc.tensor.matmul(psw[:, T:2 * T], wT[:, 1, :], wT[:, 2, :], start=True, stop=True).then_inc(tr_ok, 1)

                def body(i, nodes=False):
                    for u in range(8):
                        q = 8 * i + u
                        pe.wait_ge(oh_ok, q + 1)
                        for c in range(4):
                            last = nc.tensor.matmul(psc[:, 0:NB], pairl[:, u % 4, c // 2, :, c % 2], pairb[:, u % 4, c // 2, :, c % 2],
                                                    start=isinstance(i, int) and i == 0 and u == 0 and c == 0,
                                                    stop=isinstance(i, int) and i == HR - 1 and u == 7 and c == 3)
                        last.then_inc(h_used, 1)
                        if nodes and u == 2:
                            pe.wait_ge(stg_ok, i)
                            pe.sem_inc(pe_turns, 1)
                            nc.tensor.transpose(psE[:, 0, :], stage[:, 0, :], ident[:, :])
                            nc.tensor.transpose(psE[:, 1, :], stage[:, 1, :], ident[:, :]).then_inc(node_T, 1)
                        if nodes and u == 5:
                            pe.wait_ge(node_e, i)
                            nc.tensor.matmul(psQ[:, 0, :], eT[:, 0, :], wqp[:, :], start=True, stop=True)
                            nc.tensor.matmul(psQ[:, 1, :], eT[:, 1, :], wqp[:, :], start=True, stop=True).then_inc(node_m, 1)
                body(0)
                with pe.Fori(1, NB // 2 + 1) as i:
                    body(i, True)
                for i in range(NB // 2 + 1, HR):
                    body(i)
                pe.wait_ge(cnt_ok, 1)
                nc.tensor.matmul(psb[:, 0, 0:NB], trif[:, :], cnt[:, :], start=True, stop=True)
                nc.tensor.matmul(psb[:, 1, 0:NB], onesf[:, :], cnt[:, :], start=True, stop=True).then_inc(pre_ok, 1)

            @block.scalar
            def _(act):
                act.wait_ge(tr_ok, 1)
                nc.scalar.copy(wT[:, :, :].rearrange("p k c -> p (k c)"), psw[:, 0:3 * D]).then_inc(ev_ok, 1)
                act.wait_ge(tr_ok, 2)
                nc.scalar.copy(wqp[:, :], psw[:, 0:2 * T]).then_inc(wqp_ok, 1)
                act.wait_ge(wqp_ok, 1)
                act.wait_ge(loads, 16 * n_loads)
                with act.Fori(1, NB // 2 + 1) as i:
                    b = 2 * i - 2
                    nc.scalar.copy(stage[:, :, :], emb[:, bass.ds(b, 2), :]).then_inc(stg_ok, 1)
                    act.wait_ge(node_T, i)
                    nc.scalar.copy(eT[:, :, :], psE[:, 0:2, :]).then_inc(node_e, 1)
                    act.wait_ge(node_m, i)
                    nc.scalar.copy(qs[:, bass.ds(b, 2), :], psQ[:, 0:2, 0:T])
                    nc.scalar.copy(ps[:, bass.ds(b, 2), :], psQ[:, 0:2, T:2 * T]).then_inc(node_q, 1)

            @block.vector
            def _(dve):
                link = Chain(dve, dve_links)
                nc.vector.memset(raw[96:L, 2, REST:COLS], N).then_inc(pads, 1)
                nc.vector.memset(raw[96:L, 0:2, REST:COLS], 0).then_inc(pads, 1)
                dve.wait_ge(hloads, 16 * NPARTS)
                nc.vector.tensor_scalar(hint[:, 0, :], raw[:, 2, :], L - 1, None, ALU.bitwise_and)
                link(nc.vector.tensor_scalar(hint[:, 1, :], raw[:, 2, :], L.bit_length() - 1, None, ALU.logical_shift_right))
                nc.vector.tensor_copy(hl[:, :], hint[:, 0, :])
                link(nc.vector.tensor_copy(hb[:, :], hint[:, 1, :]))
                nc.vector.memset(zeros[:, :], 0.0).then_inc(z_ok, 1)
                dve.wait_ge(const, 6)

                def body(i):
                    for u in range(8):
                        q = 8 * i + u
                        if reached(q, 4):
                            dve.wait_ge(h_used, q - 3)
                        for table, digit, width in ((pairl, hl, L), (pairb, hb, NB)):
                            last = nc.vector.tensor_tensor(
                                table[:, u % 4, :, :, :], iota2[:, 0:width, :].unsqueeze(1).to_broadcast([L, 2, width, 2]),
                                digit[:, bass.ds(4 * q, 4)].rearrange("p (a c) -> p a c", c=2).unsqueeze(2).to_broadcast([L, 2, width, 2]),
                                ALU.is_equal)
                        last.then_inc(oh_ok, 1)
                rounds(dve, link, HR, 0, body)
                nc.vector.tensor_copy(identb[:, :], ident[:, :])
                nc.vector.tensor_copy(trib[:, :], trif[:, :])
                dve.wait_ge(h_used, Q4)
                nc.vector.tensor_copy(cnt[:, :], psc[:, 0:NB]).then_inc(cnt_ok, 1)
                link(nc.vector.memset(tot1[:, 0:1], 1.0))
                dve.wait_ge(pre_ok, 1)
                link(nc.vector.tensor_copy(tot[:, :], psb[:, 1, 0:NB]))
                link(nc.vector.tensor_tensor_scan(tot1[:, 1:NB + 1], onesf[:, 0:NB], tot[:, :], tot1[:, 0:1], ALU.mult, ALU.add))
                link(nc.vector.tensor_tensor(base[:, :], psb[:, 0, 0:NB], tot1[:, 0:NB], ALU.add))
                link(nc.vector.tensor_copy(ring_r[:, 3, 3, :], base[:, :]))
                chain_at["dve"] = link.n

        def one_hots(q, r):
            nc.vector.tensor_tensor(ohl[:, r, :, :], iotab[:, :].unsqueeze(1).to_broadcast([L, 4, L]),
                                    hl[:, bass.ds(4 * q, 4)].unsqueeze(2).to_broadcast([L, 4, L]), ALU.is_equal)
            return nc.vector.tensor_tensor(ohb[:, r, :, :], iotab[:, 0:NB].unsqueeze(1).to_broadcast([L, 4, NB]),
                                           hb[:, bass.ds(4 * q, 4)].unsqueeze(2).to_broadcast([L, 4, NB]), ALU.is_equal)

        with ExitStack() as s3:
            oTb = sb(s3, "oTb", [L, 4, 4, L], bf16)
            oTc = sb(s3, "oTc", [NB, 4, 4, L], bf16)
            oTf = sb(s3, "oTf", [L, 4, 4, L])
            prior = sb(s3, "prior", [L, 2, 4, L], bf16)
            masked = sb(s3, "masked", [L, 4, NB])
            rank = sb(s3, "rank", [L, 4])
            rankix = sb(s3, "rankix", [L, 2, 16], i32)
            recst = sb(s3, "recst", [L, 2, 16, 3], i32)
            psT = [pb(s3, f"psT{k}", [L, 2, 4, L], bf16) for k in range(2)]
            psS = [pb(s3, f"psS{k}", [L, 4, L]) for k in range(2)]
            psG = [pb(s3, f"psG{k}", [L, 4, L]) for k in range(2)]
            psH = [pb(s3, f"psH{k}", [L, 4, L]) for k in range(2)]
            oh2, t_ok, h_ok, same_ok, g_ok, oT_ok, r_ok, s_ok, m_ok, grp_ok = (sem(n) for n in (
                "oh2", "t_ok", "h_ok", "same_ok", "g_ok", "oT_ok", "r_ok", "s_ok", "m_ok", "grp_ok"))
            scat = [sem(f"scat{k}") for k in range(2)]
            RR = Q4 // 8
            block = s3.enter_context(nc.Block())

            @block.vector
            def _(dve):
                link = Chain(dve, dve_links, chain_at["dve"])

                def counts(q, u):
                    dve.wait_ge(h_ok, q + 1)
                    if reached(q, 1):
                        dve.wait_ge(r_ok, q)
                    nc.vector.tensor_tensor(ring_r[:, u % 4, :, :], psH[u % 2][:, :, 0:NB],
                                            ring_r[:, (u - 1) % 4, 3:4, :].to_broadcast([L, 4, NB]), ALU.add).then_inc(r_ok, 1)

                def priors(q, u):
                    dve.wait_ge(same_ok, q + 1)
                    nc.vector.scalar_tensor_tensor(prior[:, u % 2, :, :], psS[u % 2][:, :, :], 2.0,
                                                   trib[:, :].unsqueeze(1).to_broadcast([L, 4, L]),
                                                   ALU.is_equal, ALU.mult).then_inc(s_ok, 1)

                def ranks(q, u, rounds_done):
                    par, k = (u // 4) % 2, u % 4
                    if k == 0:
                        if reached(q, 8):
                            dve.wait_ge(scat[par], rounds_done)
                        nc.vector.tensor_copy(recst[:, par, :, :].rearrange("p c k -> p (c k)"),
                                              recc[:, bass.ds(4 * q, 16), :].rearrange("p c k -> p (c k)"))
                    dve.wait_ge(g_ok, q + 1)
                    link(nc.vector.tensor_tensor(masked[:, :, :], psG[u % 2][:, :, 0:NB], ohb[:, u % 4, :, :], ALU.mult))
                    m_ok_ins = nc.vector.tensor_reduce(rank[:, :], masked[:, :, :], AX.X, ALU.add)
                    m_ok_ins.then_inc(m_ok, 1)
                    dve.wait_ge(m_ok, q + 1)
                    last = nc.vector.tensor_copy(rankix[:, par, 4 * k:4 * k + 4], rank[:, :])
                    if k == 3:
                        last.then_inc(grp_ok, 1)

                def body(i):
                    for u in range(8):
                        q = 8 * i + u
                        one_hots(q, u % 4).then_inc(oh2, 1)
                        if reached(q, 1):
                            counts(q - 1, u - 1)
                        if reached(q, 2):
                            priors(q - 2, u - 2)
                        if reached(q, 3):
                            ranks(q - 3, u - 3, 256 * i)

                rounds(dve, link, RR, 8, body)
                counts(Q4 - 1, 7)
                priors(Q4 - 2, 6)
                ranks(Q4 - 3, 5, None)
                priors(Q4 - 1, 7)
                ranks(Q4 - 2, 6, None)
                ranks(Q4 - 1, 7, None)
                chain_at["dve"] = link.n

            @block.tensor
            def _(pe):
                def flip(q, u):
                    pe.wait_ge(oh2, q + 1)
                    for c in range(4):
                        nc.tensor.transpose(psT[u % 2][:, 0, c, :], ohl[:, u % 4, c, :], identb[:, :])
                        last = nc.tensor.transpose(psT[u % 2][0:NB, 1, c, :], ohb[:, u % 4, c, :], identb[:, :])
                    last.then_inc(t_ok, 1)

                def hist(q, u):
                    if reached(q, 2):
                        pe.wait_ge(r_ok, q - 1)
                    for c in range(4):
                        for b in range(c + 1):
                            last = nc.tensor.matmul(psH[u % 2][:, c, 0:NB], ohl[:, u % 4, b, :], ohb[:, u % 4, b, :],
                                                    start=b == 0, stop=b == c)
                    last.then_inc(h_ok, 1)

                def same(q, u):
                    pe.wait_ge(oT_ok, q + 1)
                    for c in range(4):
                        nc.tensor.matmul(psS[u % 2][:, c, :], oTb[:, u % 4, c, :], oTb[:, u % 4, c, :], start=True, stop=False)
                        last = nc.tensor.matmul(psS[u % 2][:, c, :], oTc[:, u % 4, c, :], oTc[:, u % 4, c, :], start=False, stop=True)
                    last.then_inc(same_ok, 1)

                def candidates(q, u):
                    pe.wait_ge(s_ok, q + 1)
                    pe.wait_ge(r_ok, q + 1)
                    if reached(q, 2):
                        pe.wait_ge(m_ok, q - 1)
                    for c in range(4):
                        r = ring_r[:, u % 4, c - 1, :] if c else ring_r[:, (u - 1) % 4, 3, :]
                        nc.tensor.matmul(psG[u % 2][:, c, 0:NB], oTf[:, u % 4, c, :], r, start=True, stop=False)
                        last = nc.tensor.matmul(psG[u % 2][:, c, 0:NB], prior[:, u % 2, c, :], ohb[:, u % 4, c, :], start=False, stop=True)
                    last.then_inc(g_ok, 1)

                def body(i):
                    for u in range(8):
                        q = 8 * i + u
                        flip(q, u)
                        hist(q, u)
                        if reached(q, 1):
                            same(q - 1, u - 1)
                        if reached(q, 2):
                            candidates(q - 2, u - 2)
                body(0)
                with pe.Fori(1, RR) as i:
                    body(i)
                same(Q4 - 1, 7)
                candidates(Q4 - 2, 6)
                candidates(Q4 - 1, 7)

            @block.scalar
            def _(act):
                def body(i):
                    for u in range(8):
                        q = 8 * i + u
                        act.wait_ge(t_ok, q + 1)
                        if reached(q, 4):
                            act.wait_ge(g_ok, q - 3)
                        nc.scalar.copy(oTb[:, u % 4, :, :], psT[u % 2][:, 0, :, :])
                        nc.scalar.copy(oTc[:, u % 4, :, :], psT[u % 2][0:NB, 1, :, :])
                        nc.scalar.copy(oTf[:, u % 4, :, :], psT[u % 2][:, 0, :, :]).then_inc(oT_ok, 1)
                body(0)
                with act.Fori(1, RR) as i:
                    body(i)

            @block.gpsimd
            def _(gp):
                with gp.Fori(0, RR) as i:
                    for g in range(2):
                        gp.wait_ge(grp_ok, 2 * i + g + 1)
                        gp.sem_inc(turns, 1)
                        for c in range(16):
                            nc.gpsimd.indirect_dma_start(
                                rec, bass.IndirectOffsetOnAxis(ap=rankix[:, g, c:c + 1], axis=0),
                                recst[:, g, c, :], None, bounds_check=EP, oob_is_err=False).then_inc(scat[g], 16)
                for g in range(2):
                    gp.wait_ge(scat[g], 256 * RR)
                gp.wait_ge(x_zero, 16 * ZR)
        early.close()

        with ExitStack() as s4:
            recs = sb(s4, "recs", [L, COLS + 1, 3], i32)
            jota = sb(s4, "jota", [L, COLS])
            m1 = sb(s4, "m1", [L, 4])
            cut = sb(s4, "cut", [L, S])
            psx = pb(s4, "psx", [L, L])
            rl, jo, cut_ok, cutT_ok = (sem(n) for n in ("rl", "jo", "cut_ok", "cutT_ok"))
            block = s4.enter_context(nc.Block())

            @block.sync
            def _(sp):
                sp.dma_start(recs[:, 0:COLS, :], rec[0:EP, :].rearrange("(p j) k -> p j k", p=L)).then_inc(rl, 16)
                sp.dma_start(recs[:, COLS, :], rec[1:EP + 1, :].rearrange("(p j) k -> p j k", p=L)[:, COLS - 1, :]).then_inc(rl, 16)
                sp.wait_ge(rl, 32)

            @block.gpsimd
            def _(gp):
                nc.gpsimd.iota(jota[:, :], pattern=[[1, COLS]], base=0, channel_multiplier=0,
                               allow_small_or_imprecise_dtypes=True).then_inc(jo, 1)
                gp.wait_ge(six_ok, 1)
                gp.wait_ge(x_zero, 16 * ZR)
                for b in range(NB):
                    nc.gpsimd.indirect_dma_start(
                        x_head, bass.IndirectOffsetOnAxis(ap=startix[:, b:b + 1], axis=0), ps[:, b, :], None,
                        bounds_check=EP - 1, oob_is_err=False).then_inc(psc_sem, 16)
                gp.wait_ge(hf_ok, 1)
                nc.gpsimd.indirect_dma_start(
                    pcarry[:, :], None, pt, bass.IndirectOffsetOnAxis(ap=hfirst[:, 0:1], axis=0),
                    bounds_check=NP - 1, oob_is_err=False).then_inc(pcar, 16)
                gp.wait_ge(pcar, 16)
                gp.wait_ge(psc_sem, 16 * NB)

            @block.vector
            def _(dve):
                link = Chain(dve, dve_links, chain_at["dve"])
                link(nc.vector.tensor_scalar(has[:, :], cnt[:, :], 1.0, None, ALU.min))
                link(nc.vector.tensor_scalar(tmp3[:, :], has[:, :], -FAR, FAR - 1.0, ALU.mult, ALU.add))
                link(nc.vector.tensor_tensor(tmp3[:, :], tmp3[:, :], base[:, :], ALU.add))
                nc.vector.tensor_copy(startix[:, :], tmp3[:, :]).then_inc(six_ok, 1)
                dve.wait_ge(six_ok, 1)
                link(nc.vector.tensor_tensor(tmp3[:, :], base[:, :], cnt[:, :], ALU.add))
                link(nc.vector.tensor_scalar(tmp3[:, :], tmp3[:, :], -2.0, 0.0, ALU.add, ALU.max))
                link(nc.vector.tensor_copy(endix[:, :], tmp3[:, :]))
                dve.wait_ge(rl, 32)
                nc.vector.tensor_copy(hfirst[:, :], recs[:, 1, 2:3]).then_inc(hf_ok, 1)
                nc.vector.tensor_copy(tails[:, :], recs[:, 1:COLS + 1, 0])
                nc.vector.tensor_copy(types[:, :], recs[:, 1:COLS + 1, 1])
                link(nc.vector.tensor_tensor(keep[:, :], recs[:, 1:COLS + 1, 2], recs[:, 0:COLS, 2], ALU.is_equal))
                link(nc.vector.tensor_scalar(neg[:, :], keep[:, :], -NEG, NEG, ALU.mult, ALU.add))
                dve.wait_ge(jo, 1)
                link(nc.vector.scalar_tensor_tensor(jota[:, :], keep[:, :], float(COLS), jota[:, :], ALU.mult, ALU.add))
                link(nc.vector.tensor_reduce(m1[:, 0:1], jota[:, 1:COLS], AX.X, ALU.min))
                link(nc.vector.tensor_scalar(m1[:, 1:2], m1[:, 0:1], float(COLS), -1.0, ALU.min, ALU.add))
                link(nc.vector.tensor_tensor(m1[:, 2:3], m1[:, 1:2], pbase[:, :], ALU.add))
                link(nc.vector.tensor_copy(fixix[:, :], m1[:, 2:3]))
                link(nc.vector.tensor_reduce(m1[:, 3:4], neg[:, :], AX.X, ALU.min))
                link(nc.vector.tensor_copy(cut[:, :], m1[:, 3:4].to_broadcast([L, S])))
                nc.vector.memset(res[:, :, :], 0.0).then_inc(cut_ok, 1)
                dve.wait_ge(cutT_ok, 1)
                link(nc.vector.tensor_copy(cutT[:, :], psx[0:S, :]))
                link(nc.vector.tensor_copy(res[:, :, :], emb[:, :, :]))
                chain_at["dve"] = link.n

            @block.tensor
            def _(pe):
                pe.wait_ge(cut_ok, 1)
                nc.tensor.transpose(psx[0:S, :], cut[:, :], ident[:, :]).then_inc(cutT_ok, 1)

        tables.close()

        J = 16
        B = COLS // J
        BR = B // 4
        ix_ok, pin_ok, a_ok, ae_ok, gfree, st_ok, or_ok, m_set, z_set = (sem(n) for n in (
            "ix_ok", "pin_ok", "a_ok", "ae_ok", "gfree", "st_ok", "or_ok", "m_set", "z_set"))
        gath = [sem(f"gath{k}") for k in range(4)]
        xl = [sem(f"xl{k}") for k in range(2)]
        so = [sem(f"so{k}") for k in range(2)]
        tl_ok, tlT_ok, aw2_ok, ex2_ok, cv_ok, cvT_ok, fx, d_ok, e2_ok, fix_ok, sq_ok, sqr_ok, row_ok, sr_ok, out_ok, y_ok = (sem(n) for n in (
            "tl_ok", "tlT_ok", "aw2_ok", "ex2_ok", "cv_ok", "cvT_ok", "fx", "d_ok", "e2_ok", "fix_ok", "sq_ok", "sqr_ok", "row_ok", "sr_ok", "out_ok", "y_ok"))
        e_new, T_new, eT_new, m_new, p_new = (sem(n) for n in ("e_new", "T_new", "eT_new", "m_new", "p_new"))
        lots0 = NB // 7
        rows_ok = [sem(f"rows_ok{g}") for g in range(NB // 7)]
        NG = 7
        NS = NB // NG
        for hop in range(HOPS):
            with ExitStack() as s6:
                ix = sb(s6, f"ix{hop}", [L, 4, J], i32)
                G = sb(s6, f"G{hop}", [L, 4, J, D + T])
                Xb = sb(s6, f"Xb{hop}", [L, 2, J, T])
                Pin = sb(s6, f"Pin{hop}", [L, 2, T, J + 1])
                KE = sb(s6, f"KE{hop}", [L, 2, T, J + 1])
                Pex = sb(s6, f"Pex{hop}", [L, 2, T, J + 1])
                U = sb(s6, f"U{hop}", [L, J, T])
                OHt = sb(s6, f"OHt{hop}", [L, J, T])
                er = sb(s6, f"er{hop}", [L, J])
                el = sb(s6, f"el{hop}", [L, J])
                Mx = sb(s6, f"Mx{hop}", [L, 4, J + 1])
                dd = sb(s6, f"dd{hop}", [L, J])
                aw = sb(s6, f"aw{hop}", [L, 2, 2, J])
                ew = sb(s6, f"ew{hop}", [L, 2, 2, J])
                WR = sb(s6, f"WR{hop}", [L, V, J + 1])
                AE = sb(s6, f"AE{hop}", [L, 2, V, J + 1])
                ST = sb(s6, f"ST{hop}", [L, 2, V, J + 1])
                OR = sb(s6, f"OR{hop}", [L, 2, J, S])
                block = s6.enter_context(nc.Block())
                hb0 = hop * B
                hr0 = hop * BR
                xv = x_head.rearrange("(p j) t -> p j t", p=L)
                sv = states.rearrange("(p j) t -> p j t", p=L)

                @block.sync
                def _(sp):
                    def load(b, u, i):
                        if reached(b, 2):
                            sp.wait_ge(pin_ok, hb0 + b - 1)
                        sp.dma_start(Xb[:, u % 2, :, :], xv[:, bass.ds(b * J, J), :]).then_inc(xl[u % 2], 16)

                    def store(b, u, i):
                        sp.wait_ge(or_ok, hb0 + b + 1)
                        sp.dma_start(sv[:, bass.ds(b * J, J), :], OR[:, u % 2, :, :]).then_inc(so[u % 2], 16)
                    load(0, 0, 0)

                    def body(i, last=False):
                        for u in range(4):
                            b = 4 * i + u
                            if not (last and u == 3):
                                load(b + 1, u + 1, i)
                            if reached(b, 2):
                                store(b - 2, u - 2, i)
                    body(0)
                    with sp.Fori(1, BR - 1) as i:
                        body(i)
                    body(BR - 1, True)
                    store(B - 2, 2, 0)
                    store(B - 1, 3, 0)
                    for k in range(2):
                        sp.wait_ge(so[k], 16 * (B // 2) * (hop + 1))

                @block.gpsimd
                def _(gp):
                    def body(i):
                        for u in range(4):
                            b = 4 * i + u
                            if reached(b, 4):
                                gp.wait_ge(gfree, hb0 + b - 3)
                                gp.sem_inc(turns, 1)
                            gp.wait_ge(ix_ok, hb0 + b + 1)
                            gp.sem_inc(turns, 1)
                            for j in range(J):
                                nc.gpsimd.indirect_dma_start(
                                    G[:, u, j, :], None, tq, bass.IndirectOffsetOnAxis(ap=ix[:, u, j:j + 1], axis=0),
                                    bounds_check=NP - 1, oob_is_err=False).then_inc(gath[u], 16)
                    body(0)
                    with gp.Fori(1, BR) as i:
                        body(i)

                @block.scalar
                def _(act):
                    def pin(b, u, i):
                        act.wait_ge(xl[u % 2], 16 * (hr0 * 2 + 2 * i + u // 2 + 1))
                        nc.scalar.copy(Pin[:, u % 2, :, 1:J + 1], Xb[:, u % 2, :, :].rearrange("p j t -> p t j"))
                        nc.scalar.copy(KE[:, u % 2, :, 1:J + 1],
                                       keep[:, bass.ds(b * J, J)].unsqueeze(1).to_broadcast([L, T, J])).then_inc(pin_ok, 1)

                    def weigh(b, u):
                        act.wait_ge(a_ok, hb0 + b + 1)
                        nc.scalar.activation(ew[:, u % 2, :, :], aw[:, u % 2, :, :], ACT.Exp).then_inc(m_set, 1)
                        act.wait_ge(m_set, hb0 + b + 1)
                        nc.scalar.copy(AE[:, u % 2, :, 1:J + 1],
                                       ew[:, u % 2, 0:1, :].to_broadcast([L, V, J])).then_inc(ae_ok, 1)

                    def pack(b, u, i):
                        act.wait_ge(st_ok, hb0 + b + 1)
                        if reached(b, 2):
                            act.wait_ge(so[u % 2], 16 * (hr0 * 2 + 2 * i + u // 2))
                        nc.scalar.copy(OR[:, u % 2, :, 0:V], ST[:, u % 2, :, 1:J + 1].rearrange("p f j -> p j f"))
                        nc.scalar.copy(OR[:, u % 2, :, V], Mx[:, u % 4, 1:J + 1]).then_inc(or_ok, 1)

                    def body(i):
                        for u in range(4):
                            b = 4 * i + u
                            pin(b, u, i)
                            if reached(b, 1):
                                weigh(b - 1, u - 1)
                            if reached(b, 2):
                                pack(b - 2, u - 2, i)
                    act.wait_ge(z_set, hop + 1)
                    body(0)
                    with act.Fori(1, BR) as i:
                        body(i)
                    weigh(B - 1, 3)
                    pack(B - 2, 2, BR - 1)
                    pack(B - 1, 3, BR - 1)

                @block.vector
                def _(dve):
                    link = Chain(dve, dve_links, chain_at["dve"])

                    def stage_ix(b, u):
                        nc.vector.tensor_copy(ix[:, u % 4, :], tails[:, bass.ds(b * J, J)]).then_inc(ix_ok, 1)

                    def logits(b, u, i):
                        p, pp = u % 2, (u - 1) % 2
                        dve.wait_ge(pin_ok, hb0 + b + 1)
                        link(nc.vector.tensor_copy(Pin[:, p, :, 0:1],
                                                   Pex[:, pp, :, J:J + 1] if reached(b, 1) else pcarry[:, :].unsqueeze(2)))
                        flat = lambda a: a[:, p, :, :].rearrange("p t j -> p (t j)")
                        nc.vector.tensor_tensor_scan(flat(Pex), flat(KE), flat(Pin), 0.0, ALU.mult, ALU.add)
                        link(nc.vector.tensor_tensor(OHt[:, :, :], iotaf[:, :].unsqueeze(1).to_broadcast([L, J, T]),
                                                     types[:, bass.ds(b * J, J)].unsqueeze(2).to_broadcast([L, J, T]), ALU.is_equal))
                        dve.wait_ge(gath[u], 16 * J * (hr0 + i + 1))
                        link(nc.vector.tensor_tensor(U[:, :, :], Pex[:, p, :, 1:J + 1].rearrange("p t j -> p j t"),
                                                     G[:, u, :, D:D + T], ALU.add))
                        link(nc.vector.tensor_tensor(U[:, :, :], U[:, :, :], OHt[:, :, :], ALU.mult))
                        link(nc.vector.tensor_reduce(er[:, :], U[:, :, :], AX.X, ALU.add))
                        link(nc.vector.scalar_tensor_tensor(el[:, :], er[:, :], 0.2, er[:, :], ALU.mult, ALU.max))
                        link(nc.vector.tensor_copy(Mx[:, u, 0:1], Mx[:, (u - 1) % 4, J:J + 1]))
                        link(nc.vector.tensor_tensor_scan(Mx[:, u, 1:J + 1], neg[:, bass.ds(b * J, J)], el[:, :],
                                                          Mx[:, u, 0:1], ALU.add, ALU.max))
                        link(nc.vector.tensor_tensor(dd[:, :], Mx[:, u, 0:J], neg[:, bass.ds(b * J, J)], ALU.add))
                        nc.vector.tensor_tensor(aw[:, p, 0, :], dd[:, :], Mx[:, u, 1:J + 1], ALU.subtract)
                        nc.vector.tensor_tensor(aw[:, p, 1, :], el[:, :], Mx[:, u, 1:J + 1], ALU.subtract).then_inc(a_ok, 1)

                    def sums(b, u):
                        p, pp = u % 2, (u - 1) % 2
                        dve.wait_ge(ae_ok, hb0 + b + 1)
                        nc.vector.tensor_tensor(WR[:, 0:D, 1:J + 1], G[:, u % 4, :, 0:D].rearrange("p j f -> p f j"),
                                                ew[:, p, 1:2, :].to_broadcast([L, D, J]), ALU.mult).then_inc(gfree, 1)
                        nc.vector.tensor_copy(WR[:, D, 1:J + 1], ew[:, p, 1, :])
                        link(nc.vector.tensor_copy(WR[:, :, 0:1], ST[:, pp, :, J:J + 1]))
                        dve.wait_ge(gfree, hb0 + b + 1)
                        flat = lambda a: a[:, p, :, :].rearrange("p t j -> p (t j)")
                        nc.vector.tensor_tensor_scan(flat(ST), flat(AE), WR[:, :, :].rearrange("p t j -> p (t j)"),
                                                     0.0, ALU.mult, ALU.add).then_inc(st_ok, 1)
                        dve.wait_ge(st_ok, hb0 + b + 1)

                    def body(i, last=False):
                        for u in range(4):
                            b = 4 * i + u
                            if not (last and u >= 2):
                                stage_ix(b + 2, u + 2)
                            logits(b, u, i)
                            if reached(b, 1):
                                sums(b - 1, u - 1)

                    stage_ix(0, 0)
                    stage_ix(1, 1)
                    nc.vector.memset(Mx[:, 3, :], NEG)
                    nc.vector.memset(ST[:, 1, :, :], 0.0)
                    for k in range(2):
                        nc.vector.memset(KE[:, k, :, 0:1], 0.0)
                        link(nc.vector.memset(AE[:, k, :, 0:1], 0.0))
                    nc.vector.memset(dd[:, 0:1], 0.0).then_inc(z_set, 1)
                    body(0)
                    before = link.n
                    LINKS = 4 * 10
                    with dve.Fori(1, BR - 1) as i:
                        link.base = (i - 1) * LINKS
                        body(i)
                        assert link.n == before + LINKS, link.n - before
                    link.n, link.base = before + (BR - 2) * LINKS, 0
                    body(BR - 1, True)
                    sums(B - 1, 3)
                    nc.vector.tensor_copy(tail_state[:, 0:V], ST[:, 1, :, J])
                    nc.vector.tensor_copy(tail_state[:, V:S], Mx[:, 3, J:J + 1])
                    link(nc.vector.memset(dd[:, 0:1], 0.0))
                    chain_at["dve"] = link.n

            with ExitStack() as s7:
                final = hop == HOPS - 1
                mbc = sb(s7, f"mbc{hop}", [L, S])
                tT = sb(s7, f"tT{hop}", [S, L])
                mT = sb(s7, f"mT{hop}", [S, L])
                MC = sb(s7, f"MC{hop}", [S, L + 1])
                CV = sb(s7, f"CV{hop}", [S, L + 1])
                aw2 = sb(s7, f"aw2{hop}", [S, 2, L])
                ew2 = sb(s7, f"ew2{hop}", [S, 2, L])
                carr = sb(s7, f"carr{hop}", [L, S])
                mcar = sb(s7, f"mcar{hop}", [L, 1])
                fr = sb(s7, f"fr{hop}", [L, S])
                mm = sb(s7, f"mm{hop}", [L, 3])
                me = sb(s7, f"me{hop}", [L, 2])
                R = sb(s7, f"R{hop}", [L, NB, S])
                tmp = sb(s7, f"tmp{hop}", [L, 2, NG, D])
                st = sb(s7, f"st{hop}", [L, 8, NB])
                eTn = sb(s7, f"eTn{hop}", [D, 2, NG, L])
                qn = sb(s7, f"qn{hop}", [L, NB, T])
                pn = sb(s7, f"pn{hop}", [L, NB, T])
                psm = pb(s7, f"psm{hop}", [L, 4, L])
                psE = pb(s7, f"psEn{hop}", [L, 8, L])
                psQ = [pb(s7, f"psQn{hop}{k}", [L, 8, 2 * T]) for k in range(2)]
                block = s7.enter_context(nc.Block())

                def part(g):
                    return slice(g * NG, (g + 1) * NG)

                @block.tensor
                def _(pe):
                    pe.wait_ge(tl_ok, hop + 1)
                    nc.tensor.transpose(psm[0:S, 0, :], tail_state[:, :], ident[:, :])
                    nc.tensor.transpose(psm[0:S, 1, :], mbc[:, :], ident[:, :]).then_inc(tlT_ok, 1)
                    pe.wait_ge(cv_ok, hop + 1)
                    nc.tensor.transpose(psm[:, 2, 0:S], CV[:, 0:L], ident[0:S, 0:S])
                    nc.tensor.transpose(psm[:, 3, 0:S], MC[:, 0:L], ident[0:S, 0:S]).then_inc(cvT_ok, 1)
                    if not final:
                        for g in range(NS):
                            pe.wait_ge(e_new, g + 1)
                            if g:
                                pe.wait_ge(eT_new, g)
                            for k in range(NG):
                                last = nc.tensor.transpose(psE[0:D, k, :], emb[:, g * NG + k, :], ident[:, :])
                            last.then_inc(T_new, 1)
                            pe.wait_ge(eT_new, g + 1)
                            if g >= 2:
                                pe.wait_ge(p_new, g - 1)
                            for k in range(NG):
                                last = nc.tensor.matmul(psQ[g % 2][:, k, :], eTn[:, g % 2, k, :], wqp[:, :], start=True, stop=True)
                            last.then_inc(m_new, 1)

                @block.scalar
                def _(act):
                    act.wait_ge(aw2_ok, hop + 1)
                    nc.scalar.activation(ew2[:, :, :], aw2[:, :, :], ACT.Exp).then_inc(ex2_ok, 1)
                    act.wait_ge(d_ok, hop + 1)
                    nc.scalar.activation(me[:, :], mm[:, 1:3], ACT.Exp).then_inc(e2_ok, 1)

                    def square(g, lot, a):
                        act.wait_ge(row_ok, lot + 1)
                        nc.scalar.activation(tmp[:, lot % 2, :, :], a[:, part(g), :], ACT.Square).then_inc(sqr_ok, 1)

                    def root(g, lot, slot):
                        act.wait_ge(sq_ok, lot + 1)
                        nc.scalar.activation(st[:, slot + 1, part(g)], st[:, slot, part(g)], ACT.Sqrt).then_inc(sr_ok, 1)

                    def tables_out(g):
                        act.wait_ge(T_new, g + 1)
                        if g >= 2:
                            act.wait_ge(m_new, g - 1)
                        nc.scalar.copy(eTn[:, g % 2, :, :], psE[0:D, 0:NG, :]).then_inc(eT_new, 1)
                        act.wait_ge(m_new, g + 1)
                        nc.scalar.copy(qn[:, part(g), :], psQ[g % 2][:, 0:NG, 0:T])
                        nc.scalar.copy(pn[:, part(g), :], psQ[g % 2][:, 0:NG, T:2 * T]).then_inc(p_new, 1)

                    for g in range(NS + 1):
                        if final:
                            if g:
                                square(g - 1, lots0 + 2 * g - 1, res)
                            if g < NS:
                                square(g, lots0 + 2 * g, emb)
                            if g:
                                root(g - 1, lots0 + 2 * g - 1, 5)
                            if g < NS:
                                root(g, lots0 + 2 * g, 1)
                        else:
                            if g < NS:
                                square(g, g, emb)
                                root(g, g, 1)
                            if g > 1:
                                tables_out(g - 2)
                    if not final:
                        tables_out(NS - 1)

                @block.gpsimd
                def _(gp):
                    nc.gpsimd.indirect_dma_start(
                        fr[:, :], None, states, bass.IndirectOffsetOnAxis(ap=fixix[:, 0:1], axis=0),
                        bounds_check=EP - 1, oob_is_err=False).then_inc(fx, 16)
                    gp.wait_ge(fix_ok, hop + 1)
                    nc.gpsimd.indirect_dma_start(
                        states, bass.IndirectOffsetOnAxis(ap=fixix[:, 0:1], axis=0), fr[:, :], None,
                        bounds_check=EP - 1, oob_is_err=False).then_inc(fx, 16)
                    gp.wait_ge(fx, 32 * (hop + 1))
                    for b in range(NB):
                        nc.gpsimd.indirect_dma_start(
                            R[:, b, :], None, states, bass.IndirectOffsetOnAxis(ap=endix[:, b:b + 1], axis=0),
                            bounds_check=EP - 1, oob_is_err=False).then_inc(rows_ok[b // NG], 16)
                    if not final:
                        for b in range(NB):
                            if b % NG == 0:
                                gp.wait_ge(p_new, b // NG + 1)
                            nc.gpsimd.indirect_dma_start(
                                x_head, bass.IndirectOffsetOnAxis(ap=startix[:, b:b + 1], axis=0), pn[:, b, :], None,
                                bounds_check=EP - 1, oob_is_err=False).then_inc(psc_sem, 16)
                        gp.wait_ge(tqw, 48 + 48 * NS)
                        nc.gpsimd.indirect_dma_start(
                            pcarry[:, :], None, pt, bass.IndirectOffsetOnAxis(ap=hfirst[:, 0:1], axis=0),
                            bounds_check=NP - 1, oob_is_err=False).then_inc(pcar, 16)
                        gp.wait_ge(pcar, 32)
                        gp.wait_ge(psc_sem, 32 * NB)

                @block.vector
                def _(dve):
                    link = Chain(dve, dve_links, chain_at["dve"])
                    nc.vector.tensor_copy(mbc[:, :], tail_state[:, V:S].to_broadcast([L, S])).then_inc(tl_ok, 1)
                    dve.wait_ge(tlT_ok, hop + 1)
                    nc.vector.tensor_copy(tT[:, :], psm[0:S, 0, :])
                    nc.vector.tensor_copy(mT[:, :], psm[0:S, 1, :])
                    nc.vector.memset(CV[:, 0:1], 0.0)
                    link(nc.vector.memset(MC[:, 0:1], NEG))
                    link(nc.vector.tensor_tensor_scan(MC[:, 1:L + 1], cutT[:, :], mT[:, :], MC[:, 0:1], ALU.add, ALU.max))
                    link(nc.vector.tensor_tensor(aw2[:, 0, :], MC[:, 0:L], cutT[:, :], ALU.add))
                    link(nc.vector.tensor_tensor(aw2[:, 0, :], aw2[:, 0, :], MC[:, 1:L + 1], ALU.subtract))
                    nc.vector.tensor_tensor(aw2[:, 1, :], mT[:, :], MC[:, 1:L + 1], ALU.subtract).then_inc(aw2_ok, 1)
                    dve.wait_ge(ex2_ok, hop + 1)
                    link(nc.vector.tensor_tensor(tT[:, :], tT[:, :], ew2[:, 1, :], ALU.mult))
                    nc.vector.tensor_tensor_scan(CV[:, 1:L + 1], ew2[:, 0, :], tT[:, :], CV[:, 0:1], ALU.mult, ALU.add).then_inc(cv_ok, 1)
                    dve.wait_ge(cvT_ok, hop + 1)
                    nc.vector.tensor_copy(carr[:, :], psm[:, 2, 0:S])
                    link(nc.vector.tensor_tensor(mcar[:, :], psm[:, 3, 0:1], neg[:, 0:1], ALU.add))
                    dve.wait_ge(fx, 32 * hop + 16)
                    link(nc.vector.tensor_tensor(mm[:, 0:1], fr[:, V:S], mcar[:, :], ALU.max))
                    nc.vector.tensor_tensor(mm[:, 1:2], fr[:, V:S], mm[:, 0:1], ALU.subtract)
                    nc.vector.tensor_tensor(mm[:, 2:3], mcar[:, :], mm[:, 0:1], ALU.subtract).then_inc(d_ok, 1)
                    dve.wait_ge(e2_ok, hop + 1)
                    link(nc.vector.tensor_scalar(carr[:, 0:V], carr[:, 0:V], me[:, 1:2], None, ALU.mult))
                    link(nc.vector.scalar_tensor_tensor(fr[:, 0:V], fr[:, 0:V], me[:, 0:1], carr[:, 0:V], ALU.mult, ALU.add))
                    nc.vector.tensor_copy(fr[:, V:S], mm[:, 0:1]).then_inc(fix_ok, 1)

                    def over(col, g):
                        return st[:, col, part(g)].unsqueeze(2).to_broadcast([L, NG, D])

                    def flat(a, g):
                        return a[:, part(g), :].rearrange("p b d -> p (b d)")

                    def gather(g):
                        dve.wait_ge(rows_ok[g], 16 * NG * (hop + 1))
                        link(nc.vector.reciprocal(st[:, 0, part(g)], R[:, part(g), D]))
                        link(nc.vector.tensor_tensor(st[:, 0, part(g)], st[:, 0, part(g)], has[:, part(g)], ALU.mult))
                        link(nc.vector.tensor_tensor(R[:, part(g), 0:D], R[:, part(g), 0:D], over(0, g), ALU.mult))
                        nc.vector.tensor_tensor(emb[:, part(g), :], emb[:, part(g), :], R[:, part(g), 0:D], ALU.add).then_inc(row_ok, 1)

                    def sum_up(g, lot, scale, low, op):
                        dve.wait_ge(sqr_ok, lot + 1)
                        link(nc.vector.tensor_reduce(st[:, 3, part(g)], tmp[:, lot % 2, :, :], AX.X, ALU.add))
                        nc.vector.tensor_scalar(st[:, 5 if op == ALU.add else 1, part(g)], st[:, 3, part(g)], scale, low, ALU.mult, op).then_inc(sq_ok, 1)

                    def unit(g, lot):
                        dve.wait_ge(sr_ok, lot + 1)
                        link(nc.vector.reciprocal(st[:, 0, part(g)], st[:, 2, part(g)]))
                        last = nc.vector.tensor_tensor(emb[:, part(g), :], emb[:, part(g), :], over(0, g), ALU.mult)
                        last.then_inc(e_new, 1)
                        dve.wait_ge(e_new, hop * NS + g + 1)
                        link(nc.vector.scalar_tensor_tensor(flat(res, g), flat(res, g), 0.5 if final else 2.5,
                                                            flat(emb, g), ALU.mult, ALU.add))

                    def center(g):
                        link(nc.vector.tensor_reduce(st[:, 4, part(g)], res[:, part(g), :], AX.X, ALU.add))
                        link(nc.vector.tensor_scalar(st[:, 4, part(g)], st[:, 4, part(g)], 1.0 / D, None, ALU.mult))
                        nc.vector.tensor_tensor(res[:, part(g), :], res[:, part(g), :], over(4, g), ALU.subtract).then_inc(row_ok, 1)

                    def normal(g, lot):
                        dve.wait_ge(sr_ok, lot + 1)
                        link(nc.vector.reciprocal(st[:, 7, part(g)], st[:, 6, part(g)]))
                        nc.vector.tensor_tensor(res[:, part(g), :], res[:, part(g), :], over(7, g), ALU.mult).then_inc(out_ok, 1)

                    if final:
                        for g in range(NS + 1):
                            lot = lots0 + 2 * g
                            if g < NS:
                                gather(g)
                            if g:
                                sum_up(g - 1, lot - 1, 1.0 / D, 1e-5, ALU.add)
                            if g < NS:
                                sum_up(g, lot, 1.0, 1e-24, ALU.max)
                            if g:
                                normal(g - 1, lot - 1)
                            if g < NS:
                                unit(g, lot)
                                center(g)
                    else:
                        for g in range(NS + 1):
                            if g < NS:
                                gather(g)
                            if g:
                                unit(g - 1, g - 1)
                            if g < NS:
                                sum_up(g, g, 1.0, 1e-24, ALU.max)
                    chain_at["dve"] = link.n

                @block.sync
                def _(sp):
                    if not final:
                        for g in range(NS):
                            rows = slice(g * NG * L, (g + 1) * NG * L)
                            sp.wait_ge(e_new, g + 1)
                            sp.dma_start(tq[rows, 0:D].rearrange("(b p) d -> p b d", p=L), emb[:, part(g), :]).then_inc(tqw, 16)
                            sp.wait_ge(p_new, g + 1)
                            sp.dma_start(pt[rows, :].rearrange("(b p) d -> p b d", p=L), pn[:, part(g), :]).then_inc(tqw, 16)
                            sp.dma_start(tq[rows, D:D + T].rearrange("(b p) d -> p b d", p=L), qn[:, part(g), :]).then_inc(tqw, 16)
                        sp.wait_ge(tqw, 48 + 48 * NS)
                    else:
                        for g in range(NS):
                            sp.wait_ge(out_ok, g + 1)
                            full = min((g + 1) * NG, NB - 1)
                            sp.dma_start(out[g * NG * L:full * L, :].rearrange("(b p) d -> p b d", p=L),
                                         res[:, g * NG:full, :]).then_inc(y_ok, 16)
                        sp.dma_start(out[(NB - 1) * L:N, :], res[0:NL, NB - 1, :]).then_inc(y_ok, 16)
                        sp.wait_ge(y_ok, 16 * (NS + 1))


_INS = ["x", "src", "dst", "edge_type_64", "L0_gnn_relation_emb", "L0_gnn_W"]


def kernel(**inputs):
    import numpy as _np
    import concourse.bacc as _bacc
    from concourse import mybir as _mybir
    from concourse.bass_utils import run_bass_kernel_spmd as _run

    nc = _bacc.Bacc("TRN2", target_bir_lowering=False, num_devices=1)
    arrays, args = {}, []
    for name in _INS:
        a = _np.ascontiguousarray(inputs[name])
        arrays[f"in_{name}_dram"] = a
        args.append(nc.dram_tensor(f"in_{name}_dram", a.shape, _mybir.dt.from_np(a.dtype), kind="ExternalInput").ap())
    shape = inputs["x"].shape
    out = nc.dram_tensor("out_dram", shape, _mybir.dt.float32, kind="ExternalOutput").ap()
    gnn_kernel(nc, *args, out)
    r = _run(nc, [arrays], core_ids=[0])
    return r.results[0]["out_dram"]
```

```python
import concourse.bass as bass
from concourse import mybir
from contextlib import ExitStack


def gnn_kernel(nc, x, src, dst, etype, rel, W, out):
    f32, i32, bf16 = mybir.dt.float32, mybir.dt.int32, mybir.dt.bfloat16
    ALU, ACT, AX = mybir.AluOpType, mybir.ActivationFunctionType, mybir.AxisListType

    L = 128
    N, D = x.shape
    E = src.shape[0]
    T = rel.shape[0]
    HOPS = 2
    NB = -(-(N + 1) // L)
    NP = NB * L
    COLS = -(-E // (L * 64)) * 64
    EP = L * COLS
    KB = COLS // L
    NL = N - (NB - 1) * L
    NEG = -1.0e30
    FAR = float(1 << 22)
    V = D + 1
    S = V + 1

    RW = D + T + 3
    TAIL, TYPE, HEAD = D + T, D + T + 1, D + T + 2
    rec = nc.dram_tensor("rec_sorted", [EP + 1, RW], f32, kind="Internal").ap()
    x_head = nc.dram_tensor("head_rows", [EP, T], f32, kind="Internal").ap()
    tq = nc.dram_tensor("tail_rows", [NP, D + T], f32, kind="Internal").ap()
    pt = nc.dram_tensor("p_rows", [NP, T], f32, kind="Internal").ap()
    states = nc.dram_tensor("edge_states", [EP, S], f32, kind="Internal").ap()

    ctx = ExitStack()
    with ctx:
        def sem(name):
            return ctx.enter_context(nc.semaphore(name))

        def sb(scope, name, shape, dt=f32):
            return scope.enter_context(nc.sbuf_tensor(name, shape, dt))

        def pb(scope, name, shape, dt=f32):
            return scope.enter_context(nc.psum_tensor(name, shape, dt))

        def reached(step, k):
            return not isinstance(step, int) or step >= k

        class Chain:

            def __init__(self, eng, s, start=0):
                self.eng, self.sem, self.n, self.base = eng, s, start, 0

            def __call__(self, ins):
                ins.then_inc(self.sem, 1)
                self.n += 1
                self.eng.wait_ge(self.sem, self.base + self.n)

            def mark(self, ins):
                ins.then_inc(self.sem, 1)
                self.n += 1
                return self.base + self.n

        def rounds(eng, chain, n, links, body, peel=1):
            for i in range(peel):
                body(i)
            before = chain.n
            with eng.Fori(peel, n) as i:
                chain.base = (i - peel) * links
                body(i)
                assert chain.n == before + links, chain.n - before
            chain.n, chain.base = before + (n - peel) * links, 0

        ident = sb(ctx, "ident", [L, L])
        identb = sb(ctx, "identb", [L, L], bf16)
        pcol = sb(ctx, "pcol", [L, 1])
        iotap = sb(ctx, "iotap", [L, T, 2], bf16)
        trif = sb(ctx, "trif", [L, L])
        trib = sb(ctx, "trib", [L, L], bf16)
        onesf = sb(ctx, "onesf", [L, L])
        pbase = sb(ctx, "pbase", [L, 1])
        base = sb(ctx, "base", [L, NB])
        cnt = sb(ctx, "cnt", [L, NB])
        startix = sb(ctx, "startix", [L, NB], i32)
        endix = sb(ctx, "endix", [L, NB], i32)
        has = sb(ctx, "has", [L, NB])
        emb = sb(ctx, "emb", [L, NB, D])
        wqp = sb(ctx, "wqp", [D, 2 * T])
        psc_sem, pcar, hf_ok, six_ok = sem("p_scattered"), sem("p_carried"), sem("hf_ok"), sem("six_ok")
        pcarry = sb(ctx, "pcarry", [L, T])
        tail_state = sb(ctx, "tail_state", [L, S])
        tmp3 = sb(ctx, "tmp3", [L, NB])
        tails = sb(ctx, "tails", [L, COLS], i32)
        types = sb(ctx, "types", [L, COLS], bf16)
        keep = sb(ctx, "keep", [L, COLS])
        neg = sb(ctx, "neg", [L, COLS])
        fixix = sb(ctx, "fixix", [L, 1], i32)
        hfirst = sb(ctx, "hfirst", [L, 1], i32)
        cutT = sb(ctx, "cutT", [S, L])
        res = sb(ctx, "res", [L, NB, D])

        dve_links = sem("dve_links")
        turns, pe_turns, sp_turns = sem("pool_turns"), sem("pe_turns"), sem("sp_turns")
        chain_at = {"dve": 0}

        def one_hot(table, digits, width, q, r):
            return nc.vector.tensor_tensor(
                table[:, r, :, :, :], iota2[:, 0:width, :].unsqueeze(1).to_broadcast([L, 2, width, 2]),
                digits[:, bass.ds(4 * q, 4)].rearrange("p (a c) -> p a c", c=2).unsqueeze(2).to_broadcast([L, 2, width, 2]),
                ALU.is_equal)

        tables = ExitStack()
        ps = sb(tables, "ps0", [L, NB, T])
        early = ExitStack()
        recc = sb(early, "recc", [L, 3, COLS])
        hl = sb(early, "hl", [L, COLS], bf16)
        hb = sb(early, "hb", [L, COLS], bf16)
        ub = sb(early, "ub", [L, COLS], bf16)
        t0i = sb(early, "t0i", [1, COLS // 4], i32)
        flag = sb(early, "flag", [1, 1], i32)
        before = sb(early, "before", [1, RW])
        Q4 = COLS // 4
        HR = Q4 // 8
        iota2 = sb(early, "iota2", [L, L, 2], bf16)
        pairl = sb(early, "pairl", [L, 4, 2, L, 2], bf16)
        pairb = sb(early, "pairb", [L, 4, 2, NB, 2], bf16)
        ring_r = sb(early, "ring_r", [L, 4, 4, NB])
        zeros = sb(early, "zeros", [L, 16 * T])
        ZR = COLS // 16
        x_zero = sem("x_zero")
        tqw, node_T, node_e, node_m, node_q = (sem(n) for n in ("tqw", "node_T", "node_e", "node_m", "node_q"))
        hloads, eloads, wloads, loads, const, wqp_ok = (sem(n) for n in ("hloads", "eloads", "wloads", "loads", "const", "wqp_ok"))
        n_loads = 3
        with ExitStack() as s0:
            raw = sb(s0, "raw", [L, 3, KB, L], i32)
            rawf = sb(s0, "rawf", [L, 3, KB, L])
            w1 = sb(s0, "w1", [D, 3, D])
            wT = sb(s0, "wT", [D, 3, D])
            lim = sb(s0, "lim", [L, 8])
            headi, digit = tails, res[:, :, :].rearrange("p b d -> p (b d)")[:, 0:COLS].bitcast(i32)
            t0b, uf = keep[:, 0:Q4], neg
            psA = [pb(s0, f"psA{k}", [L, 4 * L]) for k in range(4)]
            psw = pb(s0, "psw", [L, 4 * L])
            pads, rawf_ok, tr_ok, ev_ok, w_tr, w_ev, win_tr, win_ev, lim_ok, lim_tr = (sem(n) for n in (
                "pads", "rawf_ok", "tr_ok", "ev_ok", "w_tr", "w_ev", "win_tr", "win_ev", "lim_ok", "lim_tr"))
            GT = KB // 4 + 1
            full = (KB - 1) * L * L
            rows, rest = divmod(E - full, L)
            NPARTS = 2 + (rest > 0)
            WC = COLS // 4
            block = s0.enter_context(nc.Block())

            @block.sync
            def _(sp):
                def edges(k, a, s):
                    sp.dma_start(raw[:, k, 0:KB - 1, :], a[0:full].rearrange("(k c e) -> c k e", c=L, e=L)).then_inc(s, 16)
                    sp.dma_start(raw[0:rows, k, KB - 1, :], a[full:full + rows * L].rearrange("(c e) -> c e", e=L)).then_inc(s, 16)
                    if rest:
                        sp.dma_start(raw[rows:rows + 1, k, KB - 1, 0:rest], a[E - rest:E].rearrange("(c e) -> c e", c=1)).then_inc(s, 16)
                sp.wait_ge(pads, 5)
                edges(2, src, hloads)
                edges(0, dst, eloads)
                edges(1, etype, eloads)
                sp.dma_start(w1[:, 0, :], W[D:2 * D, :]).then_inc(wloads, 16)
                sp.dma_start(w1[:, 1, :], W[0:D, :]).then_inc(wloads, 16)
                sp.dma_start(w1[0:T, 2, :], rel).then_inc(wloads, 16)
                sp.dma_start(emb[:, 0:NB - 1, :], x[0:(NB - 1) * L, :].rearrange("(b p) d -> p b d", p=L)).then_inc(loads, 16)
                sp.dma_start(emb[0:NL, NB - 1, :], x[(NB - 1) * L:N, :]).then_inc(loads, 16)
                sp.dma_start(rec[0:1, :], before[:, :]).then_inc(loads, 16)

            @block.gpsimd
            def _(gp):
                nc.gpsimd.memset(raw[:, 1, KB - 1, :], 0).then_inc(pads, 1)
                for k in (0, 2):
                    nc.gpsimd.memset(raw[:, k, KB - 1, :], N).then_inc(pads, 1)
                nc.gpsimd.memset(before[:, :], -1.0).then_inc(pads, 1)
                nc.gpsimd.memset(emb[:, NB - 1, :], 0.0).then_inc(pads, 1)
                nc.gpsimd.memset(onesf[:, :], 1.0).then_inc(pads, 1)
                gp.wait_ge(pads, 6)
                nc.gpsimd.affine_select(out=ident[:, :], in_=onesf[:, :], pattern=[[-1, L]], compare_op=ALU.is_equal,
                                        fill=0.0, base=0, channel_multiplier=1).then_inc(const, 1)
                nc.gpsimd.affine_select(out=trif[:, :], in_=onesf[:, :], pattern=[[1, L]], compare_op=ALU.is_gt,
                                        fill=0.0, base=0, channel_multiplier=-1).then_inc(const, 1)
                nc.gpsimd.iota(iota2[:, :, :], pattern=[[1, L], [0, 2]], base=0, channel_multiplier=0,
                               allow_small_or_imprecise_dtypes=True).then_inc(const, 1)
                nc.gpsimd.iota(iotap[:, :, :], pattern=[[1, T], [0, 2]], base=0, channel_multiplier=0,
                               allow_small_or_imprecise_dtypes=True).then_inc(const, 1)
                nc.gpsimd.iota(pbase[:, :], pattern=[[0, 1]], base=0, channel_multiplier=COLS,
                               allow_small_or_imprecise_dtypes=True).then_inc(const, 1)
                nc.gpsimd.iota(pcol[:, :], pattern=[[0, 1]], base=0, channel_multiplier=1,
                               allow_small_or_imprecise_dtypes=True).then_inc(const, 1)

            @block.tensor
            def _(pe):
                pe.wait_ge(const, 6)
                for n, k in enumerate((2, 0, 1)):
                    pe.wait_ge(rawf_ok, n + 1)
                    for g in range(GT):
                        m = GT * n + g
                        if m >= 4:
                            pe.wait_ge(ev_ok, m - 3)
                        for t in range(4 * g, min(4 * g + 4, KB)):
                            last = nc.tensor.transpose(psA[m % 4][:, (t % 4) * L:(t % 4 + 1) * L], rawf[:, k, t, :], ident[:, :])
                        last.then_inc(tr_ok, 1)
                pe.wait_ge(wloads, 16 * 3)
                for k in range(3):
                    last = nc.tensor.transpose(psw[0:D, k * D:(k + 1) * D], w1[:, k, :], ident[0:D, 0:D])
                last.then_inc(w_tr, 1)
                pe.wait_ge(w_ev, 1)
                nc.tensor.matmul(psw[0:D, 0:T], wT[:, 0, :], wT[:, 2, :], start=True, stop=True)
                nc.tensor.matmul(psw[0:D, T:2 * T], wT[:, 1, :], wT[:, 2, :], start=True, stop=True).then_inc(w_tr, 1)
                pe.wait_ge(ev_ok, 3 * GT)
                for k in range(4):
                    nc.tensor.matmul(psA[k][:, 0:WC // 4], onesf[0:1, :], recc[0:1, 0, k * WC:(k + 1) * WC:4], start=True, stop=True).then_inc(win_tr, 1)
                pe.wait_ge(lim_ok, 1)
                pe.wait_ge(wqp_ok, 1)
                nc.tensor.matmul(psw[:, 0:1], onesf[:, :], lim[:, 4:5], start=True, stop=True).then_inc(lim_tr, 1)

            @block.scalar
            def _(act):
                for n, k in enumerate((2, 0, 1)):
                    for g in range(GT):
                        act.wait_ge(tr_ok, GT * n + g + 1)
                        w = min(4 * L, KB * L - 4 * L * g)
                        nc.scalar.copy(recc[:, k, 4 * L * g:4 * L * g + w], psA[(GT * n + g) % 4][:, 0:w]).then_inc(ev_ok, 1)
                act.wait_ge(w_tr, 1)
                nc.scalar.copy(wT[:, :, :].rearrange("p k c -> p (k c)"), psw[0:D, 0:3 * D]).then_inc(w_ev, 1)
                act.wait_ge(w_tr, 2)
                nc.scalar.copy(wqp[:, :], psw[0:D, 0:2 * T]).then_inc(wqp_ok, 1)

            @block.vector
            def _(dve):
                link = Chain(dve, dve_links)
                dve.wait_ge(hloads, 16 * NPARTS)
                nc.vector.tensor_copy(rawf[:, 2, :, :], raw[:, 2, :, :]).then_inc(rawf_ok, 1)
                dve.wait_ge(eloads, 16 * 2 * NPARTS)
                nc.vector.tensor_copy(rawf[:, 0, :, :], raw[:, 0, :, :]).then_inc(rawf_ok, 1)
                nc.vector.tensor_copy(rawf[:, 1, :, :], raw[:, 1, :, :]).then_inc(rawf_ok, 1)
                dve.wait_ge(const, 6)
                nc.vector.tensor_copy(identb[:, :], ident[:, :])
                nc.vector.tensor_copy(trib[:, :], trif[:, :])
                dve.wait_ge(ev_ok, GT)
                link(nc.vector.tensor_copy(headi[:, :], recc[:, 2, :]))
                link(nc.vector.tensor_scalar(digit, headi[:, :], L - 1, None, ALU.bitwise_and))
                link(nc.vector.tensor_copy(hl[:, :], digit))
                link(nc.vector.tensor_scalar(digit, headi[:, :], L.bit_length() - 1, None, ALU.logical_shift_right))
                link(nc.vector.tensor_copy(hb[:, :], digit))
                for k in range(4):
                    dve.wait_ge(win_tr, k + 1)
                    last = nc.vector.tensor_scalar(t0b[:, k * WC // 4:(k + 1) * WC // 4], psA[k][:, 0:WC // 4], float(NP - L), None, ALU.min)
                link(last)
                nc.vector.tensor_copy(t0i[:, :], t0b[0:1, :])
                link(nc.vector.tensor_tensor(uf[:, :].rearrange("p (q c) -> p q c", c=4), recc[:, 0, :].rearrange("p (q c) -> p q c", c=4),
                                             t0b[:, :].unsqueeze(2).to_broadcast([L, Q4, 4]), ALU.subtract))
                link(nc.vector.tensor_reduce(lim[:, 0:1], uf[:, :], AX.X, ALU.min))
                link(nc.vector.tensor_reduce(lim[:, 1:2], uf[:, :], AX.X, ALU.max))
                link(nc.vector.tensor_scalar(lim[:, 2:3], lim[:, 0:1], 0.0, None, ALU.is_ge))
                link(nc.vector.tensor_scalar(lim[:, 3:4], lim[:, 1:2], float(L), None, ALU.is_lt))
                nc.vector.tensor_tensor(lim[:, 4:5], lim[:, 2:3], lim[:, 3:4], ALU.mult).then_inc(lim_ok, 1)
                dve.wait_ge(lim_tr, 1)
                link(nc.vector.tensor_scalar(lim[:, 5:6], psw[:, 0:1], L - 0.5, None, ALU.is_ge))
                nc.vector.tensor_copy(flag[:, :], lim[0:1, 5:6])
                link(nc.vector.tensor_scalar(lim[:, 6:7], lim[:, 5:6], -1.0, 1.0, ALU.mult, ALU.add))
                link(nc.vector.tensor_tensor(lim[:, 7:8], lim[:, 6:7], pcol[:, :], ALU.mult))
                link(nc.vector.tensor_scalar(ub[:, :], uf[:, :], lim[:, 5:6], lim[:, 7:8], ALU.mult, ALU.add))
                chain_at["dve"] = link.n

        with ExitStack() as s1:
            tot = sb(s1, "tot", [L, NB])
            tot1 = sb(s1, "tot1", [L, NB + 1])
            stage = sb(s1, "stage", [L, 2, D])
            eT = sb(s1, "eT", [D, 2, L])
            qs = res
            psc = pb(s1, "psc", [L, 4 * L])
            psb = pb(s1, "psb", [L, 4, L])
            psE = pb(s1, "psE", [D, 4, L])
            psQ = pb(s1, "psQ", [L, 4, 2 * T])
            z_ok, oh_ok, h_used, cnt_ok, pre_ok, stg_ok = (sem(n) for n in ("z_ok", "oh_ok", "h_used", "cnt_ok", "pre_ok", "stg_ok"))
            block = s1.enter_context(nc.Block())
            xz = x_head.rearrange("(p j) t -> p (j t)", p=L)

            @block.sync
            def _(sp):
                sp.wait_ge(z_ok, 1)
                with sp.Fori(0, ZR) as i:
                    sp.dma_start(xz[:, bass.ds(i * 16 * T, 16 * T)], zeros[:, :]).then_inc(x_zero, 16)
                sp.wait_ge(loads, 16 * n_loads)
                sp.dma_start(tq[:, 0:D].rearrange("(b p) d -> p b d", p=L), emb[:, :, :]).then_inc(tqw, 16)
                sp.wait_ge(node_q, NB // 2)
                sp.dma_start(pt.rearrange("(b p) d -> p b d", p=L), ps[:, :, :]).then_inc(tqw, 16)
                sp.dma_start(tq[:, D:D + T].rearrange("(b p) d -> p b d", p=L), qs[:, :, :]).then_inc(tqw, 16)
                sp.wait_ge(tqw, 48)

            @block.tensor
            def _(pe):
                def body(i, nodes=False):
                    for u in range(8):
                        q = 8 * i + u
                        pe.wait_ge(oh_ok, q + 1)
                        for c in range(4):
                            last = nc.tensor.matmul(psc[:, 0:NB], pairl[:, u % 4, c // 2, :, c % 2], pairb[:, u % 4, c // 2, :, c % 2],
                                                    start=isinstance(i, int) and i == 0 and u == 0 and c == 0,
                                                    stop=isinstance(i, int) and i == HR - 1 and u == 7 and c == 3)
                        last.then_inc(h_used, 1)
                        if nodes and u == 2:
                            pe.wait_ge(stg_ok, i)
                            pe.sem_inc(pe_turns, 1)
                            nc.tensor.transpose(psE[:, 0, :], stage[:, 0, :], ident[:, :])
                            nc.tensor.transpose(psE[:, 1, :], stage[:, 1, :], ident[:, :]).then_inc(node_T, 1)
                        if nodes and u == 5:
                            pe.wait_ge(node_e, i)
                            nc.tensor.matmul(psQ[:, 0, :], eT[:, 0, :], wqp[:, :], start=True, stop=True)
                            nc.tensor.matmul(psQ[:, 1, :], eT[:, 1, :], wqp[:, :], start=True, stop=True).then_inc(node_m, 1)
                body(0)
                with pe.Fori(1, NB // 2 + 1) as i:
                    body(i, True)
                for i in range(NB // 2 + 1, HR):
                    body(i)
                pe.wait_ge(cnt_ok, 1)
                nc.tensor.matmul(psb[:, 0, 0:NB], trif[:, :], cnt[:, :], start=True, stop=True)
                nc.tensor.matmul(psb[:, 1, 0:NB], onesf[:, :], cnt[:, :], start=True, stop=True).then_inc(pre_ok, 1)

            @block.scalar
            def _(act):
                act.wait_ge(loads, 16 * n_loads)
                with act.Fori(1, NB // 2 + 1) as i:
                    b = 2 * i - 2
                    nc.scalar.copy(stage[:, :, :], emb[:, bass.ds(b, 2), :]).then_inc(stg_ok, 1)
                    act.wait_ge(node_T, i)
                    nc.scalar.copy(eT[:, :, :], psE[:, 0:2, :]).then_inc(node_e, 1)
                    act.wait_ge(node_m, i)
                    nc.scalar.copy(qs[:, bass.ds(b, 2), :], psQ[:, 0:2, 0:T])
                    nc.scalar.copy(ps[:, bass.ds(b, 2), :], psQ[:, 0:2, T:2 * T]).then_inc(node_q, 1)

            @block.vector
            def _(dve):
                link = Chain(dve, dve_links, chain_at["dve"])
                nc.vector.memset(zeros[:, :], 0.0).then_inc(z_ok, 1)

                def body(i):
                    for u in range(8):
                        q = 8 * i + u
                        if reached(q, 4):
                            dve.wait_ge(h_used, q - 3)
                        one_hot(pairl, hl, L, q, u % 4)
                        one_hot(pairb, hb, NB, q, u % 4).then_inc(oh_ok, 1)
                rounds(dve, link, HR, 0, body)
                dve.wait_ge(h_used, Q4)
                nc.vector.tensor_copy(cnt[:, :], psc[:, 0:NB]).then_inc(cnt_ok, 1)
                link(nc.vector.memset(tot1[:, 0:1], 1.0))
                dve.wait_ge(pre_ok, 1)
                link(nc.vector.tensor_copy(tot[:, :], psb[:, 1, 0:NB]))
                link(nc.vector.tensor_tensor_scan(tot1[:, 1:NB + 1], onesf[:, 0:NB], tot[:, :], tot1[:, 0:1], ALU.mult, ALU.add))
                link(nc.vector.tensor_tensor(base[:, :], psb[:, 0, 0:NB], tot1[:, 0:NB], ALU.add))
                link(nc.vector.tensor_copy(ring_r[:, 3, 3, :], base[:, :]))
                chain_at["dve"] = link.n

        with ExitStack() as s3:
            scratch = res[:, :, :].rearrange("p b d -> p (b d)")
            RB = 16 * L

            def ring(k):
                return scratch[:, k * RB:(k + 1) * RB].rearrange("p (q c e) -> p q c e", q=4, c=4)
            oTf, oTt, win = ring(0), ring(1), ring(2)
            pairt = sb(s3, "pairt", [L, 4, 2, L, 2], bf16)
            oTb = sb(s3, "oTb", [L, 4, 4, L], bf16)
            oTc = sb(s3, "oTc", [NB, 4, 4, L], bf16)
            prior = sb(s3, "prior", [L, 2, 4, L], bf16)
            masked = sb(s3, "masked", [L, 4, NB])
            rank = sb(s3, "rank", [L, 4])
            rankix = sb(s3, "rankix", [L, 4, 8], i32)
            tix = sb(s3, "tix", [L, 2, 16], i32)
            recst = sb(s3, "recst", [L, 4, 8, RW])
            psT = [pb(s3, f"psT{k}", [L, 2, 4, L], bf16) for k in range(2)]
            psU = pb(s3, "psU", [L, 2, 4, L], bf16)
            psS = pb(s3, "psS", [L, 4, L])
            psG = pb(s3, "psG", [L, 4, L])
            psH = pb(s3, "psH", [L, 4, L])
            psR = [pb(s3, f"psR{k}", [L, 4, D + T]) for k in range(2)]
            oh2, t_ok, h_ok, same_ok, g_ok, oT_ok, r_ok, s_ok, m_ok, grp_ok, tix_ok, rmm_ok, row_out, dve_turns = (sem(n) for n in (
                "oh2", "t_ok", "h_ok", "same_ok", "g_ok", "oT_ok", "r_ok", "s_ok", "m_ok", "grp_ok", "tix_ok", "rmm_ok", "row_out", "dve_turns"))
            win_ok = [sem(f"win_ok{k}") for k in range(4)]
            scat = [sem(f"scat{k}") for k in range(4)]
            OUT = 8 * 16
            RR = Q4 // 8
            block = s3.enter_context(nc.Block())

            @block.sync
            def _(sp):
                def windows(i):
                    for u in range(8):
                        q = 8 * i + u
                        if reached(q, 4):
                            sp.wait_ge(rmm_ok, q - 3)
                            sp.sem_inc(sp_turns, 1)
                        t0 = sp.value_load(t0i[0:1, bass.ds(q, 1)], min_val=0, max_val=NP - L)
                        sp.dma_start(win[:, u % 4, 0, :], tq[bass.ds(t0, L), :]).then_inc(win_ok[u % 4], 16)
                fits = sp.alloc_register("fits_sp")
                sp.reg_load(fits, flag[0:1, 0:1])
                with sp.If_eq(fits, 1):
                    windows(0)
                    with sp.Fori(1, RR) as i:
                        windows(i)
                with sp.Else():
                    sp.sem_inc(sp_turns, 1)

            @block.gpsimd
            def _(gp):
                def rows_in(q, u):
                    if reached(q, 4):
                        gp.wait_ge(rmm_ok, q - 3)
                        gp.sem_inc(turns, 1)
                    for c in range(4):
                        nc.gpsimd.indirect_dma_start(
                            win[:, u % 4, c, :], None, tq,
                            bass.IndirectOffsetOnAxis(ap=tix[:, (u // 4) % 2, 4 * (u % 4) + c:4 * (u % 4) + c + 1], axis=0),
                            bounds_check=NP - 1, oob_is_err=False).then_inc(win_ok[u % 4], 16)

                def scatter(g, n):
                    gp.wait_ge(row_out, 2 * n + 2)
                    gp.sem_inc(turns, 1)
                    gp.wait_ge(grp_ok, n + 1)
                    gp.sem_inc(turns, 1)
                    for c in range(8):
                        nc.gpsimd.indirect_dma_start(
                            rec, bass.IndirectOffsetOnAxis(ap=rankix[:, g, c:c + 1], axis=0),
                            recst[:, g, c, :], None, bounds_check=EP, oob_is_err=False).then_inc(scat[g], 16)

                def both(i):
                    for h in range(2):
                        gp.wait_ge(tix_ok, 2 * i + h + 1)
                        gp.sem_inc(turns, 1)
                        for u in range(4 * h, 4 * h + 4):
                            rows_in(8 * i + u, u)
                        if h:
                            scatter(0, 4 * i)
                            scatter(1, 4 * i + 1)
                        elif reached(i, 1):
                            scatter(2, 4 * i - 2)
                            scatter(3, 4 * i - 1)
                fits = gp.alloc_register("fits_pool")
                gp.reg_load(fits, flag[0:1, 0:1])
                with gp.If_eq(fits, 1):
                    with gp.Fori(0, RR) as i:
                        for g in range(4):
                            scatter(g, 4 * i + g)
                with gp.Else():
                    both(0)
                    with gp.Fori(1, RR) as i:
                        both(i)
                    scatter(2, 4 * RR - 2)
                    scatter(3, 4 * RR - 1)
                for g in range(4):
                    gp.wait_ge(scat[g], OUT * RR)
                gp.wait_ge(x_zero, 16 * ZR)

            @block.vector
            def _(dve):
                link = Chain(dve, dve_links, chain_at["dve"])

                def counts(q, u):
                    dve.wait_ge(h_ok, q + 1)
                    if reached(q, 1):
                        dve.wait_ge(r_ok, q)
                    nc.vector.tensor_tensor(ring_r[:, u % 4, :, :], psH[:, :, 0:NB],
                                            ring_r[:, (u - 1) % 4, 3:4, :].to_broadcast([L, 4, NB]), ALU.add).then_inc(r_ok, 1)

                def priors(q, u):
                    dve.wait_ge(same_ok, q + 1)
                    nc.vector.scalar_tensor_tensor(prior[:, u % 2, :, :], psS[:, :, :], 2.0,
                                                   trib[:, :].unsqueeze(1).to_broadcast([L, 4, L]),
                                                   ALU.is_equal, ALU.mult).then_inc(s_ok, 1)

                def ranks(q, u, i):
                    g, k = (u // 2) % 4, u % 2
                    if k == 0:
                        if reached(q, 8):
                            dve.wait_ge(scat[g], OUT * (i + u // 8))
                            dve.sem_inc(dve_turns, 1)
                        nc.vector.tensor_copy(recst[:, g, :, TAIL:RW], recc[:, :, bass.ds(4 * q, 8)].rearrange("p k c -> p c k"))
                    dve.wait_ge(g_ok, q + 1)
                    link(nc.vector.tensor_tensor(masked[:, :, :].rearrange("p (a c) v -> p a c v", c=2),
                                                 psG[:, :, 0:NB].rearrange("p (a c) v -> p a c v", c=2),
                                                 pairb[:, u % 4, :, :, :].rearrange("p a v c -> p a c v"), ALU.mult))
                    nc.vector.tensor_reduce(rank[:, :], masked[:, :, :], AX.X, ALU.add).then_inc(m_ok, 1)
                    dve.wait_ge(m_ok, q + 1)
                    last = nc.vector.tensor_copy(rankix[:, g, 4 * k:4 * k + 4], rank[:, :])
                    if k == 1:
                        last.then_inc(grp_ok, 1)

                def body(i):
                    for u in range(8):
                        q = 8 * i + u
                        if u % 4 == 0:
                            if reached(q, 8):
                                dve.wait_ge(rmm_ok, q - 4)
                                dve.sem_inc(dve_turns, 1)
                            nc.vector.tensor_copy(tix[:, u // 4, :], recc[:, 0, bass.ds(4 * q, 16)]).then_inc(tix_ok, 1)
                        one_hot(pairl, hl, L, q, u % 4)
                        one_hot(pairb, hb, NB, q, u % 4)
                        one_hot(pairt, ub, L, q, u % 4).then_inc(oh2, 1)
                        if reached(q, 1):
                            counts(q - 1, u - 1)
                        if reached(q, 2):
                            priors(q - 2, u - 2)
                        if reached(q, 3):
                            ranks(q - 3, u - 3, i)

                rounds(dve, link, RR, 8, body, 2)
                counts(Q4 - 1, 7)
                priors(Q4 - 2, 6)
                ranks(Q4 - 3, 5, RR - 1)
                priors(Q4 - 1, 7)
                ranks(Q4 - 2, 6, RR - 1)
                ranks(Q4 - 1, 7, RR - 1)
                chain_at["dve"] = link.n

            @block.tensor
            def _(pe):
                def pair(table, u, c):
                    return table[:, u % 4, c // 2, :, c % 2]

                def flip(q, u):
                    pe.wait_ge(oh2, q + 1)
                    if reached(q, 1):
                        pe.wait_ge(oT_ok, q)
                    for c in range(4):
                        nc.tensor.transpose(psT[u % 2][:, 0, c, :], pair(pairl, u, c), identb[:, :])
                        nc.tensor.transpose(psT[u % 2][0:NB, 1, c, :], pair(pairb, u, c), identb[:, :])
                        last = nc.tensor.transpose(psU[:, 0, c, :], pair(pairt, u, c), identb[:, :])
                    last.then_inc(t_ok, 1)

                def hist(q, u):
                    if reached(q, 1):
                        pe.wait_ge(r_ok, q)
                    for c in range(4):
                        for b in range(c + 1):
                            last = nc.tensor.matmul(psH[:, c, 0:NB], pair(pairl, u, b), pair(pairb, u, b), start=b == 0, stop=b == c)
                    last.then_inc(h_ok, 1)

                def same(q, u):
                    pe.wait_ge(oT_ok, q + 1)
                    if reached(q, 1):
                        pe.wait_ge(s_ok, q)
                    for c in range(4):
                        nc.tensor.matmul(psS[:, c, :], oTb[:, u % 4, c, :], oTb[:, u % 4, c, :], start=True, stop=False)
                        last = nc.tensor.matmul(psS[:, c, :], oTc[:, u % 4, c, :], oTc[:, u % 4, c, :], start=False, stop=True)
                    last.then_inc(same_ok, 1)

                def rows_of(q, u, n, fit):
                    pe.wait_ge(win_ok[u % 4], (16 if fit else 64) * n)
                    if reached(q, 2):
                        pe.wait_ge(row_out, q - 1)
                    for c in range(4):
                        last = nc.tensor.matmul(psR[u % 2][:, c, :], oTt[:, u % 4, c, :], win[:, u % 4, 0 if fit else c, :], start=True, stop=True)
                    last.then_inc(rmm_ok, 1)

                def candidates(q, u):
                    pe.wait_ge(s_ok, q + 1)
                    pe.wait_ge(r_ok, q + 1)
                    if reached(q, 1):
                        pe.wait_ge(m_ok, q)
                    for c in range(4):
                        r = ring_r[:, u % 4, c - 1, :] if c else ring_r[:, (u - 1) % 4, 3, :]
                        nc.tensor.matmul(psG[:, c, 0:NB], oTf[:, u % 4, c, :], r, start=True, stop=False)
                        last = nc.tensor.matmul(psG[:, c, 0:NB], prior[:, u % 2, c, :], pair(pairb, u, c), start=False, stop=True)
                    last.then_inc(g_ok, 1)

                def program(fit):
                    def body(i):
                        for u in range(8):
                            q = 8 * i + u
                            flip(q, u)
                            hist(q, u)
                            if reached(q, 1):
                                same(q - 1, u - 1)
                                rows_of(q - 1, u - 1, 2 * i + (u - 1) // 4 + 1, fit)
                            if reached(q, 2):
                                candidates(q - 2, u - 2)
                    body(0)
                    with pe.Fori(1, RR) as i:
                        body(i)
                    same(Q4 - 1, 7)
                    rows_of(Q4 - 1, 7, 2 * RR, fit)
                    candidates(Q4 - 2, 6)
                    candidates(Q4 - 1, 7)
                fits = pe.alloc_register("fits_pe")
                pe.reg_load(fits, flag[0:1, 0:1])
                with pe.If_eq(fits, 1):
                    program(True)
                with pe.Else():
                    program(False)

            @block.scalar
            def _(act):
                def rows_out(q, u, i):
                    g, k = (u // 2) % 4, u % 2
                    act.wait_ge(rmm_ok, q + 1)
                    if k == 0 and reached(q, 8):
                        act.wait_ge(scat[g], OUT * (i + u // 8))
                    nc.scalar.copy(recst[:, g, 4 * k:4 * k + 4, 0:D + T], psR[u % 2][:, :, :]).then_inc(row_out, 1)

                def body(i):
                    for u in range(8):
                        q = 8 * i + u
                        act.wait_ge(t_ok, q + 1)
                        if reached(q, 4):
                            act.wait_ge(g_ok, q - 3)
                            act.wait_ge(rmm_ok, q - 3)
                        nc.scalar.copy(oTb[:, u % 4, :, :], psT[u % 2][:, 0, :, :])
                        nc.scalar.copy(oTc[:, u % 4, :, :], psT[u % 2][0:NB, 1, :, :])
                        nc.scalar.copy(oTf[:, u % 4, :, :], psT[u % 2][:, 0, :, :])
                        nc.scalar.copy(oTt[:, u % 4, :, :], psU[:, 0, :, :]).then_inc(oT_ok, 1)
                        if reached(q, 2):
                            rows_out(q - 2, u - 2, i)
                body(0)
                body(1)
                with act.Fori(2, RR) as i:
                    body(i)
                rows_out(Q4 - 2, 6, RR - 1)
                rows_out(Q4 - 1, 7, RR - 1)
        early.close()

        seg_sum, cut_ok, cutT_ok = sem("seg_sum"), sem("cut_ok"), sem("cutT_ok")
        with ExitStack() as s4:
            hff = sb(s4, "hff", [L, 3])
            rl = sem("rl")
            block = s4.enter_context(nc.Block())

            @block.sync
            def _(sp):
                sp.dma_start(hff[:, :], rec[1:EP + 1, :].rearrange("(p j) k -> p j k", p=L)[:, 0, TAIL:RW]).then_inc(rl, 16)

            @block.gpsimd
            def _(gp):
                gp.wait_ge(six_ok, 1)
                for b in range(NB):
                    nc.gpsimd.indirect_dma_start(
                        x_head, bass.IndirectOffsetOnAxis(ap=startix[:, b:b + 1], axis=0), ps[:, b, :], None,
                        bounds_check=EP - 1, oob_is_err=False).then_inc(psc_sem, 16)
                gp.wait_ge(hf_ok, 1)
                nc.gpsimd.indirect_dma_start(
                    pcarry[:, :], None, pt, bass.IndirectOffsetOnAxis(ap=hfirst[:, 0:1], axis=0),
                    bounds_check=NP - 1, oob_is_err=False).then_inc(pcar, 16)
                gp.wait_ge(pcar, 16)
                gp.wait_ge(psc_sem, 16 * NB)

            @block.vector
            def _(dve):
                link = Chain(dve, dve_links, chain_at["dve"])
                link(nc.vector.tensor_scalar(has[:, :], cnt[:, :], 1.0, None, ALU.min))
                link(nc.vector.tensor_scalar(tmp3[:, :], has[:, :], -FAR, FAR - 1.0, ALU.mult, ALU.add))
                link(nc.vector.tensor_tensor(tmp3[:, :], tmp3[:, :], base[:, :], ALU.add))
                nc.vector.tensor_copy(startix[:, :], tmp3[:, :]).then_inc(six_ok, 1)
                dve.wait_ge(six_ok, 1)
                link(nc.vector.tensor_tensor(tmp3[:, :], base[:, :], cnt[:, :], ALU.add))
                link(nc.vector.tensor_scalar(tmp3[:, :], tmp3[:, :], -2.0, 0.0, ALU.add, ALU.max))
                link(nc.vector.tensor_copy(endix[:, :], tmp3[:, :]))
                dve.wait_ge(rl, 16)
                nc.vector.tensor_copy(hfirst[:, :], hff[:, 2:3]).then_inc(hf_ok, 1)
                link(nc.vector.tensor_copy(res[:, :, :], emb[:, :, :]))
                chain_at["dve"] = link.n
        tables.close()

        J = 16
        B = COLS // J
        BR = B // 4
        ix_ok, pin_ok, a_ok, ae_ok, gfree, st_ok, or_ok, m_set, z_set = (sem(n) for n in (
            "ix_ok", "pin_ok", "a_ok", "ae_ok", "gfree", "st_ok", "or_ok", "m_set", "z_set"))
        pex_ok, u_ok = sem("pex_ok"), sem("u_ok")
        gath = [sem(f"gath{k}") for k in range(4)]
        recl = [sem(f"recl{k}") for k in range(4)]
        seg_ok, prevh = sem("seg_ok"), sem("prevh")
        xl = [sem(f"xl{k}") for k in range(2)]
        so = [sem(f"so{k}") for k in range(2)]
        tl_ok, tlT_ok, aw2_ok, ex2_ok, cv_ok, cvT_ok, fx, d_ok, e2_ok, fix_ok, sq_ok, sqr_ok, row_ok, sr_ok, out_ok, y_ok = (sem(n) for n in (
            "tl_ok", "tlT_ok", "aw2_ok", "ex2_ok", "cv_ok", "cvT_ok", "fx", "d_ok", "e2_ok", "fix_ok", "sq_ok", "sqr_ok", "row_ok", "sr_ok", "out_ok", "y_ok"))
        e_new, T_new, eT_new, m_new, p_new = (sem(n) for n in ("e_new", "T_new", "eT_new", "m_new", "p_new"))
        lots0 = NB // 7
        rows_ok = [sem(f"rows_ok{g}") for g in range(NB // 7)]
        NG = 7
        NS = NB // NG
        for hop in range(HOPS):
            with ExitStack() as s6:
                ix = sb(s6, f"ix{hop}", [L, 4, J], i32)
                sorted_rows = hop == 0
                G = sb(s6, f"G{hop}", [L, 4, J, RW if sorted_rows else D + T])
                Xb = sb(s6, f"Xb{hop}", [L, 2, J, T])
                Pin = sb(s6, f"Pin{hop}", [L, 2, T, J + 1])
                KE = sb(s6, f"KE{hop}", [L, 2, T, J + 1])
                Pex = sb(s6, f"Pex{hop}", [L, 2, T, J + 1])
                U = sb(s6, f"U{hop}", [L, 2, J, T])
                OHt = sb(s6, f"OHt{hop}", [L, J // 2, T, 2], bf16)
                er = sb(s6, f"er{hop}", [L, J])
                el = sb(s6, f"el{hop}", [L, J])
                Mx = sb(s6, f"Mx{hop}", [L, 4, J + 1])
                dd = sb(s6, f"dd{hop}", [L, J])
                aw = sb(s6, f"aw{hop}", [L, 2, 2, J])
                ew = sb(s6, f"ew{hop}", [L, 2, 2, J])
                WR = sb(s6, f"WR{hop}", [L, V, J + 1])
                AE = sb(s6, f"AE{hop}", [L, 2, V, J + 1])
                ST = sb(s6, f"ST{hop}", [L, 2, V, J + 1])
                OR = sb(s6, f"OR{hop}", [L, 2, J, S])
                if sorted_rows:
                    jota = sb(s6, "jota", [L, COLS])
                    m1 = sb(s6, "m1", [L, 4])
                    cut = sb(s6, "cut", [L, S])
                    psx = pb(s6, "psx", [L, 4 * L])
                block = s6.enter_context(nc.Block())
                rv = rec[1:EP + 1, :].rearrange("(p j) k -> p j k", p=L)
                hb0 = hop * B
                hr0 = hop * BR
                xv = x_head.rearrange("(p j) t -> p j t", p=L)
                sv = states.rearrange("(p j) t -> p j t", p=L)

                @block.sync
                def _(sp):
                    def load(b, u, i):
                        if reached(b, 2):
                            sp.wait_ge(pin_ok, hb0 + b - 1)
                            sp.sem_inc(sp_turns, 1)
                        sp.dma_start(Xb[:, u % 2, :, :], xv[:, bass.ds(b * J, J), :]).then_inc(xl[u % 2], 16)

                    def store(b, u, i):
                        sp.wait_ge(or_ok, hb0 + b + 1)
                        sp.sem_inc(sp_turns, 1)
                        sp.dma_start(sv[:, bass.ds(b * J, J), :], OR[:, u % 2, :, :]).then_inc(so[u % 2], 16)

                    def records(b, u):
                        if reached(b, 4):
                            sp.wait_ge(gfree, hb0 + b - 3)
                            sp.sem_inc(sp_turns, 1)
                        sp.dma_start(G[:, u % 4, :, :], rv[:, bass.ds(b * J, J), :]).then_inc(recl[u % 4], 16)
                    if sorted_rows:
                        sp.dma_start(G[:, 3, J - 1, TAIL:RW], rec[0:EP, :].rearrange("(p j) k -> p j k", p=L)[:, 0, TAIL:RW]).then_inc(prevh, 16)
                        for b in range(3):
                            records(b, b)
                    for b in range(3):
                        load(b, b, 0)

                    def body(i, last=False):
                        for u in range(4):
                            b = 4 * i + u
                            if not (last and u >= 1):
                                load(b + 3, u + 3, i)
                                if sorted_rows:
                                    records(b + 3, u + 3)
                            if reached(b, 2):
                                store(b - 2, u - 2, i)
                    body(0)
                    with sp.Fori(1, BR - 1) as i:
                        body(i)
                    body(BR - 1, True)
                    store(B - 2, 2, 0)
                    store(B - 1, 3, 0)
                    for k in range(2):
                        sp.wait_ge(so[k], 16 * (B // 2) * (hop + 1))

                @block.gpsimd
                def _(gp):
                    def tail_logits(b, u):
                        gp.wait_ge(pex_ok, b + 1)
                        gp.sem_inc(turns, 1)
                        if reached(b, 2):
                            gp.wait_ge(a_ok, b - 1)
                            gp.sem_inc(turns, 1)
                        nc.gpsimd.tensor_tensor(U[:, u % 2, :, :], Pex[:, u % 2, :, 1:J + 1].rearrange("p t j -> p j t"),
                                                G[:, u % 4, :, D:D + T], ALU.add).then_inc(u_ok, 1)

                    def weighted(b, u):
                        gp.wait_ge(m_set, b + 1)
                        gp.sem_inc(turns, 1)
                        if reached(b, 1):
                            gp.wait_ge(st_ok, b)
                            gp.sem_inc(turns, 1)
                        nc.gpsimd.tensor_tensor(WR[:, 0:D, 1:J + 1], G[:, u % 4, :, 0:D].rearrange("p j f -> p f j"),
                                                ew[:, u % 2, 1:2, :].to_broadcast([L, D, J]), ALU.mult).then_inc(gfree, 1)

                    def from_records(i, last=False):
                        for u in range(4):
                            b = 4 * i + u
                            if reached(b, 1):
                                weighted(b - 1, u - 1)
                            if not (last and u == 3):
                                tail_logits(b + 1, u + 1)

                    def gathers(i):
                        for u in range(4):
                            b = 4 * i + u
                            if reached(b, 4):
                                gp.wait_ge(gfree, hb0 + b - 3)
                                gp.sem_inc(turns, 1)
                            gp.wait_ge(ix_ok, b + 1)
                            gp.sem_inc(turns, 1)
                            for j in range(J):
                                nc.gpsimd.indirect_dma_start(
                                    G[:, u, j, :], None, tq, bass.IndirectOffsetOnAxis(ap=ix[:, u, j:j + 1], axis=0),
                                    bounds_check=NP - 1, oob_is_err=False).then_inc(gath[u], 16)
                    if sorted_rows:
                        nc.gpsimd.iota(jota[:, :], pattern=[[1, COLS]], base=0, channel_multiplier=0,
                                       allow_small_or_imprecise_dtypes=True).then_inc(seg_sum, 1)
                        tail_logits(0, 0)
                        from_records(0)
                        with gp.Fori(1, BR - 1) as i:
                            from_records(i)
                        from_records(BR - 1, True)
                        weighted(B - 1, 3)
                    else:
                        gathers(0)
                        with gp.Fori(1, BR) as i:
                            gathers(i)

                if sorted_rows:
                    @block.tensor
                    def _(pe):
                        pe.wait_ge(cut_ok, 1)
                        nc.tensor.transpose(psx[0:S, 0:L], cut[:, :], ident[:, :]).then_inc(cutT_ok, 1)

                @block.scalar
                def _(act):
                    def pin(b, u, i):
                        act.wait_ge(xl[u % 2], 16 * (hr0 * 2 + 2 * i + u // 2 + 1))
                        if reached(b, 2):
                            act.wait_ge(pex_ok, hb0 + b - 1)
                        if sorted_rows:
                            act.wait_ge(seg_ok, b + 1)
                            nc.scalar.copy(tails[:, bass.ds(b * J, J)], G[:, u % 4, :, TAIL])
                            nc.scalar.copy(types[:, bass.ds(b * J, J)], G[:, u % 4, :, TYPE])
                        nc.scalar.copy(Pin[:, u % 2, :, 1:J + 1], Xb[:, u % 2, :, :].rearrange("p j t -> p t j"))
                        nc.scalar.copy(KE[:, u % 2, :, 1:J + 1],
                                       keep[:, bass.ds(b * J, J)].unsqueeze(1).to_broadcast([L, T, J])).then_inc(pin_ok, 1)

                    def weigh(b, u):
                        act.wait_ge(a_ok, hb0 + b + 1)
                        nc.scalar.activation(ew[:, u % 2, :, :], aw[:, u % 2, :, :], ACT.Exp).then_inc(m_set, 1)
                        act.wait_ge(m_set, hb0 + b + 1)
                        nc.scalar.copy(AE[:, u % 2, :, 1:J + 1],
                                       ew[:, u % 2, 0:1, :].to_broadcast([L, V, J])).then_inc(ae_ok, 1)

                    def pack(b, u, i):
                        act.wait_ge(st_ok, hb0 + b + 1)
                        if reached(b, 2):
                            act.wait_ge(so[u % 2], 16 * (hr0 * 2 + 2 * i + u // 2))
                        nc.scalar.copy(OR[:, u % 2, :, 0:V], ST[:, u % 2, :, 1:J + 1].rearrange("p f j -> p j f"))
                        nc.scalar.copy(OR[:, u % 2, :, V], Mx[:, u % 4, 1:J + 1]).then_inc(or_ok, 1)

                    def body(i, last=False):
                        for u in range(4):
                            b = 4 * i + u
                            if reached(b, 1):
                                weigh(b - 1, u - 1)
                            if not (last and u >= 2):
                                pin(b + 2, u + 2, i)
                            if reached(b, 2):
                                pack(b - 2, u - 2, i)
                    act.wait_ge(z_set, hop + 1)
                    pin(0, 0, 0)
                    pin(1, 1, 0)
                    body(0)
                    with act.Fori(1, BR - 1) as i:
                        body(i)
                    body(BR - 1, True)
                    weigh(B - 1, 3)
                    pack(B - 2, 2, BR - 1)
                    pack(B - 1, 3, BR - 1)

                @block.vector
                def _(dve):
                    link = Chain(dve, dve_links, chain_at["dve"])

                    def stage_ix(b, u):
                        if sorted_rows:
                            return
                        nc.vector.tensor_copy(ix[:, u % 4, :], tails[:, bass.ds(b * J, J)]).then_inc(ix_ok, 1)

                    def starts(b, step, i):
                        u = step % 4
                        dve.wait_ge(recl[u], 16 * (i + step // 4 + 1))
                        nc.vector.tensor_tensor(keep[:, bass.ds(b * J, 1)], G[:, u, 0:1, HEAD], G[:, (u - 1) % 4, J - 1:J, HEAD], ALU.is_equal)
                        return nc.vector.tensor_tensor(keep[:, bass.ds(b * J + 1, J - 1)], G[:, u, 1:J, HEAD], G[:, u, 0:J - 1, HEAD], ALU.is_equal)

                    def lows(b):
                        nc.vector.tensor_scalar(neg[:, bass.ds(b * J, J)], keep[:, bass.ds(b * J, J)], -NEG, NEG, ALU.mult, ALU.add).then_inc(seg_ok, 1)

                    def carry(b, u):
                        dve.wait_ge(pin_ok, hb0 + b + 1)
                        if reached(b, 1):
                            dve.wait_ge(pex_ok, hb0 + b)
                        return nc.vector.tensor_copy(Pin[:, u % 2, :, 0:1],
                                                     Pex[:, (u - 1) % 2, :, J:J + 1] if reached(b, 1) else pcarry[:, :].unsqueeze(2))

                    def expand(b, u):
                        flat = lambda a: a[:, u % 2, :, :].rearrange("p t j -> p (t j)")
                        nc.vector.tensor_tensor_scan(flat(Pex), flat(KE), flat(Pin), 0.0, ALU.mult, ALU.add).then_inc(pex_ok, 1)

                    def entries(b, u):
                        dve.wait_ge(ae_ok, hb0 + b + 1)
                        if reached(b, 1):
                            dve.wait_ge(st_ok, hb0 + b)
                        nc.vector.tensor_copy(WR[:, D, 1:J + 1], ew[:, u % 2, 1, :])
                        return nc.vector.tensor_copy(WR[:, :, 0:1], ST[:, (u - 1) % 2, :, J:J + 1])

                    def sums(b, u):
                        p = u % 2
                        if not sorted_rows:
                            nc.vector.tensor_tensor(WR[:, 0:D, 1:J + 1], G[:, u % 4, :, 0:D].rearrange("p j f -> p f j"),
                                                    ew[:, p, 1:2, :].to_broadcast([L, D, J]), ALU.mult).then_inc(gfree, 1)
                        dve.wait_ge(gfree, hb0 + b + 1)
                        flat = lambda a: a[:, p, :, :].rearrange("p t j -> p (t j)")
                        nc.vector.tensor_tensor_scan(flat(ST), flat(AE), WR[:, :, :].rearrange("p t j -> p (t j)"),
                                                     0.0, ALU.mult, ALU.add).then_inc(st_ok, 1)

                    def step(b, u, i, ahead, behind):
                        p = u % 2
                        one_hots = nc.vector.tensor_tensor(
                            OHt[:, :, :, :], iotap[:, :, :].unsqueeze(1).to_broadcast([L, J // 2, T, 2]),
                            types[:, bass.ds(b * J, J)].rearrange("p (a c) -> p a c", c=2).unsqueeze(2).to_broadcast([L, J // 2, T, 2]),
                            ALU.is_equal)
                        link(carry(b + 1, u + 1) if ahead >= 1 else one_hots)
                        if sorted_rows:
                            dve.wait_ge(u_ok, b + 1)
                        else:
                            dve.wait_ge(gath[u], 16 * J * (i + 1))
                            link(nc.vector.tensor_tensor(U[:, p, :, :], Pex[:, p, :, 1:J + 1].rearrange("p t j -> p j t"),
                                                         G[:, u, :, D:D + T], ALU.add))
                        pairs = U[:, p, :, :].rearrange("p (a c) t -> p a c t", c=2)
                        link(nc.vector.tensor_tensor(pairs, pairs, OHt[:, :, :, :].rearrange("p a t c -> p a c t"), ALU.mult))
                        nc.vector.tensor_copy(Mx[:, u, 0:1], Mx[:, (u - 1) % 4, J:J + 1])
                        raw_logits = link.mark(nc.vector.tensor_reduce(er[:, :], U[:, p, :, :], AX.X, ALU.add))
                        if ahead >= 1:
                            expand(b + 1, u + 1)
                        if sorted_rows and ahead >= 2:
                            starts(b + 2, u + 2, i)
                        dve.wait_ge(dve_links, raw_logits)
                        link(nc.vector.scalar_tensor_tensor(el[:, :], er[:, :], 0.2, er[:, :], ALU.mult, ALU.max))
                        if sorted_rows and ahead >= 2:
                            lows(b + 2)
                        link(nc.vector.tensor_tensor_scan(Mx[:, u, 1:J + 1], neg[:, bass.ds(b * J, J)], el[:, :],
                                                          Mx[:, u, 0:1], ALU.add, ALU.max))
                        if behind:
                            entries(b - 1, u - 1)
                        link(nc.vector.tensor_tensor(dd[:, :], Mx[:, u, 0:J], neg[:, bass.ds(b * J, J)], ALU.add))
                        nc.vector.tensor_tensor(aw[:, p, 0, :], dd[:, :], Mx[:, u, 1:J + 1], ALU.subtract)
                        nc.vector.tensor_tensor(aw[:, p, 1, :], el[:, :], Mx[:, u, 1:J + 1], ALU.subtract).then_inc(a_ok, 1)
                        if behind:
                            sums(b - 1, u - 1)

                    def body(i, last=False):
                        for u in range(4):
                            b = 4 * i + u
                            if not (last and u >= 2):
                                stage_ix(b + 2, u + 2)
                            step(b, u, i, min(2, 3 - u) if last else 2, reached(b, 1))

                    stage_ix(0, 0)
                    stage_ix(1, 1)
                    nc.vector.memset(Mx[:, 3, :], NEG)
                    nc.vector.memset(ST[:, 1, :, :], 0.0)
                    for k in range(2):
                        nc.vector.memset(KE[:, k, :, 0:1], 0.0)
                        link(nc.vector.memset(AE[:, k, :, 0:1], 0.0))
                    nc.vector.memset(dd[:, 0:1], 0.0).then_inc(z_set, 1)
                    if sorted_rows:
                        dve.wait_ge(prevh, 16)
                        for b in range(2):
                            link(starts(b, b, 0))
                            lows(b)
                    link(carry(0, 0))
                    expand(0, 0)
                    body(0)
                    before = link.n
                    LINKS = 4 * (6 if sorted_rows else 7)
                    with dve.Fori(1, BR - 1) as i:
                        link.base = (i - 1) * LINKS
                        body(i)
                        assert link.n == before + LINKS, link.n - before
                    link.n, link.base = before + (BR - 2) * LINKS, 0
                    body(BR - 1, True)
                    link(entries(B - 1, 3))
                    sums(B - 1, 3)
                    dve.wait_ge(st_ok, hb0 + B)
                    nc.vector.tensor_copy(tail_state[:, 0:V], ST[:, 1, :, J])
                    nc.vector.tensor_copy(tail_state[:, V:S], Mx[:, 3, J:J + 1])
                    link(nc.vector.memset(dd[:, 0:1], 0.0))
                    if sorted_rows:
                        dve.wait_ge(seg_sum, 1)
                        link(nc.vector.scalar_tensor_tensor(jota[:, :], keep[:, :], float(COLS), jota[:, :], ALU.mult, ALU.add))
                        link(nc.vector.tensor_reduce(m1[:, 0:1], jota[:, 1:COLS], AX.X, ALU.min))
                        link(nc.vector.tensor_scalar(m1[:, 1:2], m1[:, 0:1], float(COLS), -1.0, ALU.min, ALU.add))
                        link(nc.vector.tensor_tensor(m1[:, 2:3], m1[:, 1:2], pbase[:, :], ALU.add))
                        nc.vector.tensor_copy(fixix[:, :], m1[:, 2:3])
                        link(nc.vector.tensor_reduce(m1[:, 3:4], neg[:, :], AX.X, ALU.min))
                        nc.vector.tensor_copy(cut[:, :], m1[:, 3:4].to_broadcast([L, S])).then_inc(cut_ok, 1)
                        dve.wait_ge(cutT_ok, 1)
                        link(nc.vector.tensor_copy(cutT[:, :], psx[0:S, 0:L]))
                    chain_at["dve"] = link.n

            with ExitStack() as s7:
                final = hop == HOPS - 1
                mbc = sb(s7, f"mbc{hop}", [L, S])
                tT = sb(s7, f"tT{hop}", [S, L])
                mT = sb(s7, f"mT{hop}", [S, L])
                MC = sb(s7, f"MC{hop}", [S, L + 1])
                CV = sb(s7, f"CV{hop}", [S, L + 1])
                aw2 = sb(s7, f"aw2{hop}", [S, 2, L])
                ew2 = sb(s7, f"ew2{hop}", [S, 2, L])
                carr = sb(s7, f"carr{hop}", [L, S])
                mcar = sb(s7, f"mcar{hop}", [L, 1])
                fr = sb(s7, f"fr{hop}", [L, S])
                mm = sb(s7, f"mm{hop}", [L, 3])
                me = sb(s7, f"me{hop}", [L, 2])
                R = sb(s7, f"R{hop}", [L, NB, S])
                tmp = sb(s7, f"tmp{hop}", [L, 2, NG, D])
                st = sb(s7, f"st{hop}", [L, 8, NB])
                eTn = sb(s7, f"eTn{hop}", [D, 2, NG, L])
                qn = sb(s7, f"qn{hop}", [L, NB, T])
                pn = sb(s7, f"pn{hop}", [L, NB, T])
                psm = pb(s7, f"psm{hop}", [L, 4, L])
                psE = pb(s7, f"psEn{hop}", [L, 8, L])
                psQ = [pb(s7, f"psQn{hop}{k}", [L, 8, 2 * T]) for k in range(2)]
                block = s7.enter_context(nc.Block())

                def part(g):
                    return slice(g * NG, (g + 1) * NG)

                @block.tensor
                def _(pe):
                    pe.wait_ge(tl_ok, hop + 1)
                    nc.tensor.transpose(psm[0:S, 0, :], tail_state[:, :], ident[:, :])
                    nc.tensor.transpose(psm[0:S, 1, :], mbc[:, :], ident[:, :]).then_inc(tlT_ok, 1)
                    pe.wait_ge(cv_ok, hop + 1)
                    nc.tensor.transpose(psm[:, 2, 0:S], CV[:, 0:L], ident[0:S, 0:S])
                    nc.tensor.transpose(psm[:, 3, 0:S], MC[:, 0:L], ident[0:S, 0:S]).then_inc(cvT_ok, 1)
                    if not final:
                        for g in range(NS):
                            pe.wait_ge(e_new, g + 1)
                            if g:
                                pe.wait_ge(eT_new, g)
                            for k in range(NG):
                                last = nc.tensor.transpose(psE[0:D, k, :], emb[:, g * NG + k, :], ident[:, :])
                            last.then_inc(T_new, 1)
                            pe.wait_ge(eT_new, g + 1)
                            if g >= 2:
                                pe.wait_ge(p_new, g - 1)
                            for k in range(NG):
                                last = nc.tensor.matmul(psQ[g % 2][:, k, :], eTn[:, g % 2, k, :], wqp[:, :], start=True, stop=True)
                            last.then_inc(m_new, 1)

                @block.scalar
                def _(act):
                    act.wait_ge(aw2_ok, hop + 1)
                    nc.scalar.activation(ew2[:, :, :], aw2[:, :, :], ACT.Exp).then_inc(ex2_ok, 1)
                    act.wait_ge(d_ok, hop + 1)
                    nc.scalar.activation(me[:, :], mm[:, 1:3], ACT.Exp).then_inc(e2_ok, 1)

                    def square(g, lot, a):
                        act.wait_ge(row_ok, lot + 1)
                        nc.scalar.activation(tmp[:, lot % 2, :, :], a[:, part(g), :], ACT.Square).then_inc(sqr_ok, 1)

                    def root(g, lot, slot):
                        act.wait_ge(sq_ok, lot + 1)
                        nc.scalar.activation(st[:, slot + 1, part(g)], st[:, slot, part(g)], ACT.Sqrt).then_inc(sr_ok, 1)

                    def tables_out(g):
                        act.wait_ge(T_new, g + 1)
                        if g >= 2:
                            act.wait_ge(m_new, g - 1)
                        nc.scalar.copy(eTn[:, g % 2, :, :], psE[0:D, 0:NG, :]).then_inc(eT_new, 1)
                        act.wait_ge(m_new, g + 1)
                        nc.scalar.copy(qn[:, part(g), :], psQ[g % 2][:, 0:NG, 0:T])
                        nc.scalar.copy(pn[:, part(g), :], psQ[g % 2][:, 0:NG, T:2 * T]).then_inc(p_new, 1)

                    for g in range(NS + 1):
                        if final:
                            if g:
                                square(g - 1, lots0 + 2 * g - 1, res)
                            if g < NS:
                                square(g, lots0 + 2 * g, emb)
                            if g:
                                root(g - 1, lots0 + 2 * g - 1, 5)
                            if g < NS:
                                root(g, lots0 + 2 * g, 1)
                        else:
                            if g < NS:
                                square(g, g, emb)
                                root(g, g, 1)
                            if g > 1:
                                tables_out(g - 2)
                    if not final:
                        tables_out(NS - 1)

                @block.gpsimd
                def _(gp):
                    nc.gpsimd.indirect_dma_start(
                        fr[:, :], None, states, bass.IndirectOffsetOnAxis(ap=fixix[:, 0:1], axis=0),
                        bounds_check=EP - 1, oob_is_err=False).then_inc(fx, 16)
                    gp.wait_ge(fix_ok, hop + 1)
                    nc.gpsimd.indirect_dma_start(
                        states, bass.IndirectOffsetOnAxis(ap=fixix[:, 0:1], axis=0), fr[:, :], None,
                        bounds_check=EP - 1, oob_is_err=False).then_inc(fx, 16)
                    gp.wait_ge(fx, 32 * (hop + 1))
                    for b in range(NB):
                        nc.gpsimd.indirect_dma_start(
                            R[:, b, :], None, states, bass.IndirectOffsetOnAxis(ap=endix[:, b:b + 1], axis=0),
                            bounds_check=EP - 1, oob_is_err=False).then_inc(rows_ok[b // NG], 16)
                    if not final:
                        for b in range(NB):
                            if b % NG == 0:
                                gp.wait_ge(p_new, b // NG + 1)
                            nc.gpsimd.indirect_dma_start(
                                x_head, bass.IndirectOffsetOnAxis(ap=startix[:, b:b + 1], axis=0), pn[:, b, :], None,
                                bounds_check=EP - 1, oob_is_err=False).then_inc(psc_sem, 16)
                        gp.wait_ge(tqw, 48 + 48 * NS)
                        nc.gpsimd.indirect_dma_start(
                            pcarry[:, :], None, pt, bass.IndirectOffsetOnAxis(ap=hfirst[:, 0:1], axis=0),
                            bounds_check=NP - 1, oob_is_err=False).then_inc(pcar, 16)
                        gp.wait_ge(pcar, 32)
                        gp.wait_ge(psc_sem, 32 * NB)

                @block.vector
                def _(dve):
                    link = Chain(dve, dve_links, chain_at["dve"])
                    nc.vector.tensor_copy(mbc[:, :], tail_state[:, V:S].to_broadcast([L, S])).then_inc(tl_ok, 1)
                    dve.wait_ge(tlT_ok, hop + 1)
                    nc.vector.tensor_copy(tT[:, :], psm[0:S, 0, :])
                    nc.vector.tensor_copy(mT[:, :], psm[0:S, 1, :])
                    nc.vector.memset(CV[:, 0:1], 0.0)
                    link(nc.vector.memset(MC[:, 0:1], NEG))
                    link(nc.vector.tensor_tensor_scan(MC[:, 1:L + 1], cutT[:, :], mT[:, :], MC[:, 0:1], ALU.add, ALU.max))
                    link(nc.vector.tensor_tensor(aw2[:, 0, :], MC[:, 0:L], cutT[:, :], ALU.add))
                    link(nc.vector.tensor_tensor(aw2[:, 0, :], aw2[:, 0, :], MC[:, 1:L + 1], ALU.subtract))
                    nc.vector.tensor_tensor(aw2[:, 1, :], mT[:, :], MC[:, 1:L + 1], ALU.subtract).then_inc(aw2_ok, 1)
                    dve.wait_ge(ex2_ok, hop + 1)
                    link(nc.vector.tensor_tensor(tT[:, :], tT[:, :], ew2[:, 1, :], ALU.mult))
                    nc.vector.tensor_tensor_scan(CV[:, 1:L + 1], ew2[:, 0, :], tT[:, :], CV[:, 0:1], ALU.mult, ALU.add).then_inc(cv_ok, 1)
                    dve.wait_ge(cvT_ok, hop + 1)
                    nc.vector.tensor_copy(carr[:, :], psm[:, 2, 0:S])
                    link(nc.vector.tensor_tensor(mcar[:, :], psm[:, 3, 0:1], neg[:, 0:1], ALU.add))
                    dve.wait_ge(fx, 32 * hop + 16)
                    link(nc.vector.tensor_tensor(mm[:, 0:1], fr[:, V:S], mcar[:, :], ALU.max))
                    nc.vector.tensor_tensor(mm[:, 1:2], fr[:, V:S], mm[:, 0:1], ALU.subtract)
                    nc.vector.tensor_tensor(mm[:, 2:3], mcar[:, :], mm[:, 0:1], ALU.subtract).then_inc(d_ok, 1)
                    dve.wait_ge(e2_ok, hop + 1)
                    link(nc.vector.tensor_scalar(carr[:, 0:V], carr[:, 0:V], me[:, 1:2], None, ALU.mult))
                    link(nc.vector.scalar_tensor_tensor(fr[:, 0:V], fr[:, 0:V], me[:, 0:1], carr[:, 0:V], ALU.mult, ALU.add))
                    nc.vector.tensor_copy(fr[:, V:S], mm[:, 0:1]).then_inc(fix_ok, 1)

                    def over(col, g):
                        return st[:, col, part(g)].unsqueeze(2).to_broadcast([L, NG, D])

                    def flat(a, g):
                        return a[:, part(g), :].rearrange("p b d -> p (b d)")

                    def gather(g):
                        dve.wait_ge(rows_ok[g], 16 * NG * (hop + 1))
                        link(nc.vector.reciprocal(st[:, 0, part(g)], R[:, part(g), D]))
                        link(nc.vector.tensor_tensor(st[:, 0, part(g)], st[:, 0, part(g)], has[:, part(g)], ALU.mult))
                        link(nc.vector.tensor_tensor(R[:, part(g), 0:D], R[:, part(g), 0:D], over(0, g), ALU.mult))
                        nc.vector.tensor_tensor(emb[:, part(g), :], emb[:, part(g), :], R[:, part(g), 0:D], ALU.add).then_inc(row_ok, 1)

                    def sum_up(g, lot, scale, low, op):
                        dve.wait_ge(sqr_ok, lot + 1)
                        link(nc.vector.tensor_reduce(st[:, 3, part(g)], tmp[:, lot % 2, :, :], AX.X, ALU.add))
                        nc.vector.tensor_scalar(st[:, 5 if op == ALU.add else 1, part(g)], st[:, 3, part(g)], scale, low, ALU.mult, op).then_inc(sq_ok, 1)

                    def unit(g, lot):
                        dve.wait_ge(sr_ok, lot + 1)
                        link(nc.vector.reciprocal(st[:, 0, part(g)], st[:, 2, part(g)]))
                        last = nc.vector.tensor_tensor(emb[:, part(g), :], emb[:, part(g), :], over(0, g), ALU.mult)
                        last.then_inc(e_new, 1)
                        dve.wait_ge(e_new, hop * NS + g + 1)
                        link(nc.vector.scalar_tensor_tensor(flat(res, g), flat(res, g), 0.5 if final else 2.5,
                                                            flat(emb, g), ALU.mult, ALU.add))

                    def center(g):
                        link(nc.vector.tensor_reduce(st[:, 4, part(g)], res[:, part(g), :], AX.X, ALU.add))
                        link(nc.vector.tensor_scalar(st[:, 4, part(g)], st[:, 4, part(g)], 1.0 / D, None, ALU.mult))
                        nc.vector.tensor_tensor(res[:, part(g), :], res[:, part(g), :], over(4, g), ALU.subtract).then_inc(row_ok, 1)

                    def normal(g, lot):
                        dve.wait_ge(sr_ok, lot + 1)
                        link(nc.vector.reciprocal(st[:, 7, part(g)], st[:, 6, part(g)]))
                        nc.vector.tensor_tensor(res[:, part(g), :], res[:, part(g), :], over(7, g), ALU.mult).then_inc(out_ok, 1)

                    if final:
                        for g in range(NS + 1):
                            lot = lots0 + 2 * g
                            if g < NS:
                                gather(g)
                            if g:
                                sum_up(g - 1, lot - 1, 1.0 / D, 1e-5, ALU.add)
                            if g < NS:
                                sum_up(g, lot, 1.0, 1e-24, ALU.max)
                            if g:
                                normal(g - 1, lot - 1)
                            if g < NS:
                                unit(g, lot)
                                center(g)
                    else:
                        for g in range(NS + 1):
                            if g < NS:
                                gather(g)
                            if g:
                                unit(g - 1, g - 1)
                            if g < NS:
                                sum_up(g, g, 1.0, 1e-24, ALU.max)
                    chain_at["dve"] = link.n

                @block.sync
                def _(sp):
                    if not final:
                        for g in range(NS):
                            rows = slice(g * NG * L, (g + 1) * NG * L)
                            sp.wait_ge(e_new, g + 1)
                            sp.dma_start(tq[rows, 0:D].rearrange("(b p) d -> p b d", p=L), emb[:, part(g), :]).then_inc(tqw, 16)
                            sp.wait_ge(p_new, g + 1)
                            sp.dma_start(pt[rows, :].rearrange("(b p) d -> p b d", p=L), pn[:, part(g), :]).then_inc(tqw, 16)
                            sp.dma_start(tq[rows, D:D + T].rearrange("(b p) d -> p b d", p=L), qn[:, part(g), :]).then_inc(tqw, 16)
                        sp.wait_ge(tqw, 48 + 48 * NS)
                    else:
                        for g in range(NS):
                            sp.wait_ge(out_ok, g + 1)
                            full = min((g + 1) * NG, NB - 1)
                            sp.dma_start(out[g * NG * L:full * L, :].rearrange("(b p) d -> p b d", p=L),
                                         res[:, g * NG:full, :]).then_inc(y_ok, 16)
                        sp.dma_start(out[(NB - 1) * L:N, :], res[0:NL, NB - 1, :]).then_inc(y_ok, 16)
                        sp.wait_ge(y_ok, 16 * (NS + 1))


_INS = ["x", "src", "dst", "edge_type_64", "L0_gnn_relation_emb", "L0_gnn_W"]


def kernel(**inputs):
    import numpy as _np
    import concourse.bacc as _bacc
    from concourse import mybir as _mybir
    from concourse.bass_utils import run_bass_kernel_spmd as _run

    nc = _bacc.Bacc("TRN2", target_bir_lowering=False, num_devices=1)
    arrays, args = {}, []
    for name in _INS:
        a = _np.ascontiguousarray(inputs[name])
        arrays[f"in_{name}_dram"] = a
        args.append(nc.dram_tensor(f"in_{name}_dram", a.shape, _mybir.dt.from_np(a.dtype), kind="ExternalInput").ap())
    shape = inputs["x"].shape
    out = nc.dram_tensor("out_dram", shape, _mybir.dt.float32, kind="ExternalOutput").ap()
    gnn_kernel(nc, *args, out)
    r = _run(nc, [arrays], core_ids=[0])
    return r.results[0]["out_dram"]
```
